# Optimizing a Trainium2 kernel written in Bass

```python
import numpy as np
import jax
import jax.numpy as jnp

def _softmax(x, axis=-1):
    return jax.nn.softmax(x, axis=axis)
def _gelu(x):
    return jax.nn.gelu(x, approximate=True)
def _silu(x):
    return jax.nn.silu(x)
def _sigmoid(x):
    return jax.nn.sigmoid(x)
def _layernorm(x, axis=-1, eps=1e-5):
    m = jnp.mean(x, axis=axis, keepdims=True)
    v = jnp.var(x, axis=axis, keepdims=True)
    return (x - m) / jnp.sqrt(v + eps)
def _scatter_add(tgt, idx, src, axis=0):
    return tgt.at[idx].add(src)
def _segment_sum(src, seg, n):
    return jax.ops.segment_sum(src, seg, n)

kernel_name = 'mk_conv_seq_d2_conv_nhwc256_95fdbd'

def setup_inputs(seed: int = 0):
    np.random.seed(seed)
    _w = jnp.asarray
    def _rec_inputs():
        import jax
        import jax.numpy as jnp
        _gk = jax.random.key(seed)
        x = -0.0003929 + 0.9999 * jax.random.normal(jax.random.fold_in(_gk, 1), (4, 64, 256, 256), jnp.float32)
        return x
    x = _rec_inputs()
    def _L0_conv_setup():
        import jax, jax.numpy as jnp
        import numpy as np
        import math
        B, D_MODEL, EMB, ORDER, SEQ = (4, 64, 33, 64, 256)
        TARGET, FAST_PCT, SLOW_PCT = (0.01, 0.3, 1.5)

        def _pos_emb(L, emb_dim):
            t = jnp.linspace(0.0, 1.0, L)[None, :, None]
            bands = (emb_dim - 1) // 2
            t_r = jnp.linspace(0.0, L - 1.0, L)[None, :, None]
            w = 2.0 * math.pi * t_r / L
            f = jnp.linspace(0.0001, bands - 1.0, bands)[None, None]
            zc = jnp.exp(-1j * f * w)
            z = jnp.concatenate([t, zc.real, zc.imag], axis=-1)
            return (z.astype(jnp.float32), t.astype(jnp.float32))

        def _implicit_filter(z, w1, b1, w2, b2, w3, b3, wo, freq, t, deltas):
            h = jnp.sin(freq * (z @ w1 + b1))
            h = jnp.sin(freq * (h @ w2 + b2))
            h = jnp.sin(freq * (h @ w3 + b3))
            h = h @ wo
            decay = jnp.exp(-t * jnp.abs(deltas))
            return h * decay
        key = jax.random.key(seed)
        ks = jax.random.split(key, 24)
        z, _ = _pos_emb(SEQ, EMB)

        def lin(k, fan_in, fan_out):
            return jax.random.normal(k, (fan_in, fan_out), jnp.float32) / np.sqrt(fan_in)
        inp = {'x': jax.random.normal(ks[0], (B, D_MODEL, SEQ, SEQ), jnp.float32), 'z': z, 'Xw1': lin(ks[1], EMB, ORDER), 'Xb1': jax.random.normal(ks[2], (ORDER,), jnp.float32) * 0.02, 'Xw2': lin(ks[3], ORDER, ORDER), 'Xb2': jax.random.normal(ks[4], (ORDER,), jnp.float32) * 0.02, 'Xw3': lin(ks[5], ORDER, ORDER), 'Xb3': jax.random.normal(ks[6], (ORDER,), jnp.float32) * 0.02, 'Xwo': lin(ks[7], ORDER, D_MODEL), 'Xfreq': jnp.ones((1, ORDER), jnp.float32), 'Yw1': lin(ks[8], EMB, ORDER), 'Yb1': jax.random.normal(ks[9], (ORDER,), jnp.float32) * 0.02, 'Yw2': lin(ks[10], ORDER, ORDER), 'Yb2': jax.random.normal(ks[11], (ORDER,), jnp.float32) * 0.02, 'Yw3': lin(ks[12], ORDER, ORDER), 'Yb3': jax.random.normal(ks[13], (ORDER,), jnp.float32) * 0.02, 'Ywo': lin(ks[14], ORDER, D_MODEL), 'Yfreq': jnp.ones((1, ORDER), jnp.float32), 'bias': jax.random.normal(ks[15], (D_MODEL,), jnp.float32), 'L': SEQ}
        return inp
    _L0_conv_all = _L0_conv_setup()
    _L0_conv_in = {k: v for k, v in _L0_conv_all.items() if k in ('z', 'Xw1', 'Xb1', 'Xw2', 'Xb2', 'Xw3', 'Xb3', 'Xwo', 'Xfreq', 'Yw1', 'Yb1', 'Yw2', 'Yb2', 'Yw3', 'Yb3', 'Ywo', 'Yfreq', 'bias', )}
    del _L0_conv_all

    def _L1_conv_setup():
        import jax, jax.numpy as jnp
        import numpy as np
        BLOCK = 64
        EPS = 0.01
        N_ITER = 5
        STRIDE = 3

        def _isqrt_newton_schulz(A, num_iters):
            dim = A.shape[0]
            normA = jnp.linalg.norm(A)
            Y = A / normA
            I = jnp.eye(dim, dtype=A.dtype)
            Z = jnp.eye(dim, dtype=A.dtype)
            for _ in range(num_iters):
                T = 0.5 * (3.0 * I - Z @ Y)
                Y = Y @ T
                Z = T @ Z
            return Z / jnp.sqrt(normA)
        key = jax.random.key(seed)
        x = jax.random.normal(key, (32, 64, 256, 256), dtype=jnp.float32)
        return {'x': x}
    _L1_conv_all = _L1_conv_setup()
    _L1_conv_in = {k: v for k, v in _L1_conv_all.items() if k in ()}
    del _L1_conv_all

    return {
        "x": x,
        "L0_conv_z": _L0_conv_in["z"],
        "L0_conv_Xw1": _L0_conv_in["Xw1"],
        "L0_conv_Xb1": _L0_conv_in["Xb1"],
        "L0_conv_Xw2": _L0_conv_in["Xw2"],
        "L0_conv_Xb2": _L0_conv_in["Xb2"],
        "L0_conv_Xw3": _L0_conv_in["Xw3"],
        "L0_conv_Xb3": _L0_conv_in["Xb3"],
        "L0_conv_Xwo": _L0_conv_in["Xwo"],
        "L0_conv_Xfreq": _L0_conv_in["Xfreq"],
        "L0_conv_Yw1": _L0_conv_in["Yw1"],
        "L0_conv_Yb1": _L0_conv_in["Yb1"],
        "L0_conv_Yw2": _L0_conv_in["Yw2"],
        "L0_conv_Yb2": _L0_conv_in["Yb2"],
        "L0_conv_Yw3": _L0_conv_in["Yw3"],
        "L0_conv_Yb3": _L0_conv_in["Yb3"],
        "L0_conv_Ywo": _L0_conv_in["Ywo"],
        "L0_conv_Yfreq": _L0_conv_in["Yfreq"],
        "L0_conv_bias": _L0_conv_in["bias"],
    }

def reference(x, L0_conv_z, L0_conv_Xw1, L0_conv_Xb1, L0_conv_Xw2, L0_conv_Xb2, L0_conv_Xw3, L0_conv_Xb3, L0_conv_Xwo, L0_conv_Xfreq, L0_conv_Yw1, L0_conv_Yb1, L0_conv_Yw2, L0_conv_Yb2, L0_conv_Yw3, L0_conv_Yb3, L0_conv_Ywo, L0_conv_Yfreq, L0_conv_bias):
    import jax
    import jax.numpy as jnp
    def _L0_conv_ref(x, z, Xw1, Xb1, Xw2, Xb2, Xw3, Xb3, Xwo, Xfreq, Yw1, Yb1, Yw2, Yb2, Yw3, Yb3, Ywo, Yfreq, bias, L):
        import jax, jax.numpy as jnp
        import numpy as np
        import math
        B, D_MODEL, EMB, ORDER, SEQ = (4, 64, 33, 64, 256)
        TARGET, FAST_PCT, SLOW_PCT = (0.01, 0.3, 1.5)

        def _pos_emb(L, emb_dim):
            t = jnp.linspace(0.0, 1.0, L)[None, :, None]
            bands = (emb_dim - 1) // 2
            t_r = jnp.linspace(0.0, L - 1.0, L)[None, :, None]
            w = 2.0 * math.pi * t_r / L
            f = jnp.linspace(0.0001, bands - 1.0, bands)[None, None]
            zc = jnp.exp(-1j * f * w)
            z = jnp.concatenate([t, zc.real, zc.imag], axis=-1)
            return (z.astype(jnp.float32), t.astype(jnp.float32))

        def _implicit_filter(z, w1, b1, w2, b2, w3, b3, wo, freq, t, deltas):
            h = jnp.sin(freq * (z @ w1 + b1))
            h = jnp.sin(freq * (h @ w2 + b2))
            h = jnp.sin(freq * (h @ w3 + b3))
            h = h @ wo
            decay = jnp.exp(-t * jnp.abs(deltas))
            return h * decay
        d_model = x.shape[1]
        t = jnp.linspace(0.0, 1.0, L)[None, :, None].astype(jnp.float32)
        max_dec = math.log(TARGET) / FAST_PCT
        min_dec = math.log(TARGET) / SLOW_PCT
        deltas = jnp.linspace(min_dec, max_dec, d_model)[None, None].astype(jnp.float32)
        hx = _implicit_filter(z, Xw1, Xb1, Xw2, Xb2, Xw3, Xb3, Xwo, Xfreq, t, deltas)
        hy = _implicit_filter(z, Yw1, Yb1, Yw2, Yb2, Yw3, Yb3, Ywo, Yfreq, t, deltas)
        k = jnp.einsum('ijk,imk->ijmk', hx, hy)[0]
        k = jnp.transpose(k, (2, 0, 1))
        fft_size = 2 * L
        k_f = jnp.fft.rfft2(k, s=(fft_size, fft_size)) / fft_size
        u_f = jnp.fft.rfft2(x.astype(jnp.float32), s=(fft_size, fft_size))
        y = jnp.fft.irfft2(u_f * k_f, s=(fft_size, fft_size))[..., :L, :L]
        out = y + x * bias[:, None, None]
        return out.astype(x.dtype)

    def _L1_conv_ref(x):
        import jax, jax.numpy as jnp
        import numpy as np
        BLOCK = 64
        EPS = 0.01
        N_ITER = 5
        STRIDE = 3

        def _isqrt_newton_schulz(A, num_iters):
            dim = A.shape[0]
            normA = jnp.linalg.norm(A)
            Y = A / normA
            I = jnp.eye(dim, dtype=A.dtype)
            Z = jnp.eye(dim, dtype=A.dtype)
            for _ in range(num_iters):
                T = 0.5 * (3.0 * I - Z @ Y)
                Y = Y @ T
                Z = T @ Z
            return Z / jnp.sqrt(normA)
        N, C, H, W = x.shape
        B = BLOCK
        x1 = jnp.transpose(x, (1, 0, 2, 3)).reshape(B, -1)
        x1_s = x1[:, ::STRIDE ** 2]
        mean1 = jnp.mean(x1_s, axis=-1, keepdims=True)
        xc = x1 - mean1
        cov = x1_s @ x1_s.T / x1_s.shape[1] + EPS * jnp.eye(B, dtype=x.dtype)
        deconv = _isqrt_newton_schulz(cov, N_ITER)
        out = deconv @ xc
        out = jnp.transpose(out.reshape(C, N, H, W), (1, 0, 2, 3))
        return out

    def _gn(v, G=32, eps=1e-5):
        B_, H_, W_, C_ = v.shape
        g = v.reshape(B_, H_, W_, G, C_ // G)
        m = jnp.mean(g, axis=(1, 2, 4), keepdims=True)
        s = jnp.var(g, axis=(1, 2, 4), keepdims=True)
        return ((g - m) / jnp.sqrt(s + eps)).reshape(v.shape)

    def _ln_c(v, eps=1e-6):
        m = jnp.mean(v, axis=-1, keepdims=True)
        s = jnp.var(v, axis=-1, keepdims=True)
        return (v - m) / jnp.sqrt(s + eps)

    def _ln_t(v, eps=1e-5):
        m = jnp.mean(v, axis=-1, keepdims=True)
        s = jnp.var(v, axis=-1, keepdims=True)
        return (v - m) / jnp.sqrt(s + eps)

    def _to_tokens(v):
        B_, H_, W_, C_ = v.shape
        return v.reshape(B_, H_ * W_, C_)
    def _from_tokens(t, like):
        return t.reshape(like.shape)

    x = _L0_conv_ref(x, L0_conv_z, L0_conv_Xw1, L0_conv_Xb1, L0_conv_Xw2, L0_conv_Xb2, L0_conv_Xw3, L0_conv_Xb3, L0_conv_Xwo, L0_conv_Xfreq, L0_conv_Yw1, L0_conv_Yb1, L0_conv_Yw2, L0_conv_Yb2, L0_conv_Yw3, L0_conv_Yb3, L0_conv_Ywo, L0_conv_Yfreq, L0_conv_bias, 256)
    x = _L1_conv_ref(x)
    return x


_drawn_inputs = setup_inputs


def setup_inputs(seed=0):
    import zlib

    import numpy as np

    out = dict(_drawn_inputs(seed))
    spreads = {'L0_conv_Xfreq': (1.0, 0.6), 'L0_conv_Yfreq': (1.0, 0.6)}
    factors = {'L0_conv_z': 3.814,
     'L0_conv_Xw1': 3.858,
     'L0_conv_Xb1': 8.0,
     'L0_conv_Xw2': 3.776,
     'L0_conv_Xb2': 8.0,
     'L0_conv_Xw3': 3.671,
     'L0_conv_Xb3': 8.0,
     'L0_conv_Xwo': 3.584,
     'L0_conv_Yw1': 3.619,
     'L0_conv_Yb1': 8.0,
     'L0_conv_Yw2': 3.422,
     'L0_conv_Yb2': 8.0,
     'L0_conv_Yw3': 3.61,
     'L0_conv_Yb3': 8.0,
     'L0_conv_Ywo': 3.562}
    for name, (base, spread) in spreads.items():
        noise = np.random.default_rng([zlib.crc32(name.encode()), seed]).standard_normal(out[name].shape)
        drawn = base * np.exp(spread * noise) if base else spread * noise
        out[name] = jnp.asarray(drawn.astype(out[name].dtype))
    for name, factor in factors.items():
        out[name] = (out[name] * factor).astype(out[name].dtype)
    return out
```

```python
import math
from contextlib import ExitStack

import concourse.bass as bass
from concourse import mybir

F32 = mybir.dt.float32
F32R = mybir.dt.float32r
I32 = mybir.dt.int32
ALU = mybir.AluOpType
ACT = mybir.ActivationFunctionType
AX_X = mybir.AxisListType.X

P = 128
B, C, S = 4, 64, 256
EMB, ORDER = 33, 64
HB = S // P
IMG = HB * S
STRIDE = 9
GROUPS = -(-S // STRIDE)
N_SAMPLES = -(-(B * S * S) // STRIDE)
EPS = 0.01
N_ITER = 5
PAIRS = B // 2
GLEN = S + P
MAGIC = 1.5 * 2.0 ** 23
TWO_PI = 2 * math.pi
PI_HI = 6.28125
PI_MID = math.floor((TWO_PI - PI_HI) * 2.0 ** 21) / 2.0 ** 21
PI_LO = TWO_PI - PI_HI - PI_MID
PI_BELOW = 3.1415925
MIN_DEC = -math.log(0.01) / 1.5
MAX_DEC = -math.log(0.01) / 0.3

UNROLL = 4
X_SLOTS = 4
TROWS = 8
TILES = PAIRS * (P // TROWS)
T_SLOTS = 4
O_SLOTS = 2
UNITS = TROWS // 2


def conv_whiten(nc, x, zt, w1, b1, w2, b2, w3, b3, wo, freq, bias, out):
    g_dram = nc.dram_tensor("filters", [2 * C, GLEN], F32, kind="Internal").ap()
    y_dram = nc.dram_tensor("convolved", [C, P, B * IMG], F32, kind="Internal").ap()

    with ExitStack() as ctx:
        def sb(name, shape, dt=F32):
            return ctx.enter_context(nc.sbuf_tensor(name, shape, dt))

        def sem(name):
            return ctx.enter_context(nc.semaphore(name))

        XW, YW, PW = B * IMG, B * IMG, B * HB * GROUPS * STRIDE
        z_cols = (C + 1) * B * HB * GROUPS
        arena_cols = X_SLOTS * XW + 2 * YW + 2 * PW + z_cols
        arena = sb("arena", [P, arena_cols])
        at = 0
        x_sb = [arena[:, at + k * XW:at + (k + 1) * XW] for k in range(X_SLOTS)]
        at += X_SLOTS * XW
        y_sb = [arena[:, at + k * YW:at + (k + 1) * YW] for k in range(2)]
        at += 2 * YW
        masked = [arena[:, at + k * PW:at + (k + 1) * PW].rearrange("p (i w) -> p i w", i=B * HB)
                  for k in range(2)]
        at += 2 * PW
        z_sb = arena[:, at:at + z_cols].rearrange("p (c s) -> p c s", c=C + 1)
        mask_scratch = [arena[:, at + k * YW:at + (k + 1) * YW] for k in range(3)]
        TW = TROWS * IMG
        t_in = [arena[:, k * TW:(k + 1) * TW] for k in range(T_SLOTS)]
        assert T_SLOTS * TW <= at and O_SLOTS * TW <= z_cols
        t_out = [arena[:, at + k * TW:at + (k + 1) * TW] for k in range(O_SLOTS)]

        mask = sb("mask", [P, B * HB * S])
        hankel = [sb(f"hankel{k}", [P, 2, S]) for k in range(2)]
        tx = [sb(f"tx{k}", [P, S]) for k in range(2)]
        ty_hi = [sb(f"ty_hi{k}", [P, S], F32R) for k in range(2)]
        ty_lo = [sb(f"ty_lo{k}", [P, S], F32R) for k in range(2)]
        v_hi = [sb(f"v_hi{k}", [P, 2 * IMG], F32R) for k in range(2)]
        v_lo = [sb(f"v_lo{k}", [P, 2 * IMG], F32R) for k in range(2)]
        bias_sb = sb("bias_sb", [P, C])
        zt_sb = sb("zt_sb", [EMB, S])
        w1_sb = sb("w1_sb", [EMB, 2 * ORDER])
        w2_sb, w3_sb, wo_sb = (sb(n, [P, P]) for n in ("w2_sb", "w3_sb", "wo_sb"))
        col = sb("col", [P, 4])
        arg, turns, hid = sb("arg", [P, S]), sb("turns", [P, S]), sb("hid", [P, S])
        pos_i, pos, decay = sb("pos_i", [P, S], I32), sb("pos", [P, S]), sb("decay", [P, S])
        chan_i, chan = sb("chan_i", [P, 1], I32), sb("chan", [P, 1])
        rate = sb("rate", [P, 1])
        filt = sb("filt", [P, GLEN])
        ident, ident15, ident_eps = (sb(n, [P, P]) for n in ("ident", "ident15", "ident_eps"))
        halves = sb("halves", [P, P])
        cov, sq = sb("cov", [P, P]), sb("sq", [P, P])
        ym = [sb(f"ym{k}", [P, P]) for k in range(2)]
        zm = [sb(f"zm{k}", [P, P]) for k in range(2)]
        tm = sb("tm", [P, P])
        dmat = sb("dmat", [P, P])
        small = sb("small", [P, 8])

        ps = ctx.enter_context(nc.psum_tensor("ps", [P, 8, S * 2], F32))
        ps_v = [ps[:, 2 * k:2 * k + 2, :] for k in range(2)]
        ps_y = [ps[:, 4 + 2 * k:6 + 2 * k, :] for k in range(2)]

        params_loaded, w_zeroed = sem("params_loaded"), sem("w_zeroed")
        pool_step, ident_ready, mask_ready = sem("pool_step"), sem("ident_ready"), sem("mask_ready")
        pos_ready, f_mm, f_dve, f_sin = sem("pos_ready"), sem("f_mm"), sem("f_dve"), sem("f_sin")
        decay_ready, filt_ready, filt_stored = sem("decay_ready"), sem("filt_ready"), sem("filt_stored")
        x_loaded = [sem(f"x_loaded{k}") for k in range(X_SLOTS)]
        hankel_loaded = [sem(f"hankel_loaded{k}") for k in range(2)]
        flipped, ty_lo_done = sem("flipped"), sem("ty_lo_done")
        v_mm, v_hi_done, v_lo_done = sem("v_mm"), sem("v_hi_done"), sem("v_lo_done")
        y_mm, y_done, masked_done, z_done = sem("y_mm"), sem("y_done"), sem("masked_done"), sem("z_done")
        y_stored = [sem(f"y_stored{k}") for k in range(2)]
        cov_mm, n_mm, n_dve, n_act = sem("cov_mm"), sem("n_mm"), sem("n_dve"), sem("n_act")
        d_ready = sem("d_ready")
        t_loaded = [sem(f"t_loaded{k}") for k in range(T_SLOTS)]
        t_mm = [sem(f"t_mm{u}") for u in range(UNITS)]
        t_act, t_dve = sem("t_act"), sem("t_dve")
        t_stored = [sem(f"t_stored{k}") for k in range(O_SLOTS)]

        def channels(eng, step):
            n = C // UNROLL
            for cc in range(UNROLL):
                step(0, cc)
            with eng.Fori(1, n - 1) as i:
                for cc in range(UNROLL):
                    step(i, cc)
            for cc in range(UNROLL):
                step(n - 1, cc)

        def wait(eng, s, value):
            if not isinstance(value, int) or value > 0:
                eng.wait_ge(s, value)

        def channel(i, cc):
            return i * UNROLL + cc

        def known(i, c):
            return not isinstance(i, int) or 0 <= c < C

        def stored_before(t, k):
            return (t - k % O_SLOTS) * (32 // O_SLOTS)

        def tile_loop(eng, step):
            for k in range(T_SLOTS):
                step(k, k)
            with eng.Fori(1, TILES // T_SLOTS - 1) as j:
                for k in range(T_SLOTS):
                    step(j * T_SLOTS + k, k)
            for k in range(T_SLOTS):
                step(TILES - T_SLOTS + k, k)

        block = ctx.enter_context(nc.Block())

        @block.sync
        def _(sp):
            sp.dma_start(zt_sb[:], zt).then_inc(params_loaded, 16)
            sp.dma_start(w1_sb[:], w1).then_inc(params_loaded, 16)
            for j, v in enumerate((b1, b2, b3, freq)):
                sp.dma_start(col[:, j:j + 1], v).then_inc(params_loaded, 16)
            sp.dma_start(bias_sb[:], bias.to_broadcast([P, C])).then_inc(params_loaded, 16)
            sp.wait_ge(w_zeroed, 3)
            for w_sb, w in ((w2_sb, w2), (w3_sb, w3), (wo_sb, wo)):
                for k in range(2):
                    h = slice(k * ORDER, (k + 1) * ORDER)
                    sp.dma_start(w_sb[h, h], w[h, :]).then_inc(params_loaded, 16)

            def load_x(i, cc, ahead):
                c = channel(i, cc + ahead)
                if not known(i, c):
                    return
                wait(sp, y_done, PAIRS * (c - X_SLOTS) + PAIRS)
                sp.dma_start(x_sb[(cc + ahead) % X_SLOTS], x[bass.ds(c, 1), :, :].rearrange("o p n -> (o p) n")).then_inc(
                    x_loaded[(cc + ahead) % X_SLOTS], 16)

            def load_hankel(i, cc, ahead):
                c = channel(i, cc + ahead)
                if not known(i, c):
                    return
                k = (cc + ahead) % 2
                wait(sp, flipped, c - 1)
                wait(sp, ty_lo_done, c - 1)
                src = bass.AP(tensor=g_dram.tensor, offset=c * GLEN, ap=[[1, P], [C * GLEN, 2], [1, S]])
                sp.dma_start(hankel[k][:], src).then_inc(hankel_loaded[k], 16)

            def store_y(i, cc, behind):
                c = channel(i, cc - behind)
                if not known(i, c):
                    return
                k = (cc - behind) % 2
                wait(sp, y_done, PAIRS * (c + 1))
                sp.dma_start(y_dram[bass.ds(c, 1), :, :].rearrange("o p n -> (o p) n"), y_sb[k]).then_inc(y_stored[k], 16)

            for c in range(X_SLOTS - 1):
                load_x(0, 0, c)
            sp.wait_ge(filt_ready, 1)
            sp.dma_start(g_dram, filt[:]).then_inc(filt_stored, 16)
            sp.wait_ge(filt_stored, 16)
            load_hankel(0, 0, 0)
            load_hankel(0, 0, 1)

            def step(i, cc):
                load_hankel(i, cc, 2)
                load_x(i, cc, X_SLOTS - 1)
                store_y(i, cc, 1)

            channels(sp, step)
            store_y(C // UNROLL - 1, UNROLL, 1)

            for k in range(2):
                sp.wait_ge(y_stored[k], 16 * (C // 2))
            sp.wait_ge(z_done, C)
            sp.wait_ge(y_done, PAIRS * C)

            def load_tile(t, k):
                for b in range(2):
                    src = bass.AP(tensor=y_dram.tensor,
                                  offset=(t - k % PAIRS) * (TROWS * B * IMG // PAIRS) + (k % PAIRS * 2 + b) * IMG,
                                  ap=[[P * B * IMG, C], [B * IMG, TROWS], [1, IMG]])
                    sp.dma_start(t_in[k][b * C:(b + 1) * C, :].rearrange("c (r n) -> c r n", r=TROWS),
                                 src).then_inc(t_loaded[k], 16)

            def store_tile(t, k):
                for b in range(2):
                    dst = bass.AP(tensor=out.tensor,
                                  offset=(t - k % PAIRS) * (TROWS * S // PAIRS) + (k % PAIRS * 2 + b) * C * S * S,
                                  ap=[[S * S, C], [P * S, HB], [1, TROWS * S]])
                    sp.dma_start(dst, t_out[k % O_SLOTS][b * C:(b + 1) * C, :].rearrange(
                        "c (h n) -> c h n", h=HB)).then_inc(t_stored[k % O_SLOTS], 16)

            ahead = T_SLOTS - 1

            def tile(t, k):
                if not isinstance(t, int) or t + ahead < TILES:
                    wait(sp, t_mm[UNITS - 1], t)
                    load_tile(t + ahead, (k + ahead) % T_SLOTS)
                sp.wait_ge(t_act, 2 * t + 2)
                sp.wait_ge(t_dve, 2 * t + 2)
                store_tile(t, k)

            for k in range(ahead):
                load_tile(k, k)
            tile_loop(sp, tile)
            for k in range(O_SLOTS):
                sp.wait_ge(t_stored[k], 32 * (TILES // O_SLOTS))

        @block.gpsimd
        def _(pool):
            n_step = [0]

            def chained(ins):
                n_step[0] += 1
                ins.then_inc(pool_step, 1)
                pool.wait_ge(pool_step, n_step[0])

            for w_sb in (w2_sb, w3_sb, wo_sb):
                nc.gpsimd.memset(w_sb[:], 0.0).then_inc(w_zeroed, 1)
            nc.gpsimd.memset(filt[:], 0.0)
            nc.gpsimd.iota(pos_i[:], pattern=[[-1, S]], base=S - 1, channel_multiplier=0)
            chained(nc.gpsimd.iota(chan_i[:], pattern=[[0, 1]], base=0, channel_multiplier=1))
            nc.gpsimd.tensor_copy(pos[:], pos_i[:])
            nc.gpsimd.tensor_copy(chan[:], chan_i[:]).then_inc(pos_ready, 1)
            idx_i, idx, near = mask_scratch[0].bitcast(I32), mask_scratch[1], mask_scratch[2]
            chained(nc.gpsimd.iota(idx_i.rearrange("p (b h w) -> p b h w", b=B, h=HB),
                                   pattern=[[(S * S) % STRIDE, B], [(S * P) % STRIDE, HB], [1, S]],
                                   base=0, channel_multiplier=S % STRIDE))
            chained(nc.gpsimd.tensor_copy(idx, idx_i))
            chained(nc.gpsimd.tensor_scalar(near, idx, 1.0 / STRIDE, MAGIC, ALU.mult, ALU.add))
            chained(nc.gpsimd.tensor_scalar(near, near, MAGIC, float(STRIDE), ALU.subtract, ALU.mult))
            chained(nc.gpsimd.tensor_tensor(idx, idx, near, ALU.subtract))
            nc.gpsimd.tensor_scalar(mask[:], idx, 0.0, None, ALU.is_equal).then_inc(mask_ready, 1)
            for k in range(2):
                nc.gpsimd.memset(masked[k][:, :, S:], 0.0)
            chained(nc.gpsimd.memset(ident[:], 0.0))
            chained(nc.gpsimd.affine_select(out=ident[:], in_=ident[:], compare_op=ALU.not_equal, fill=1.0,
                                            base=0, pattern=[[-1, P]], channel_multiplier=1))
            nc.gpsimd.tensor_scalar(ident15[:], ident[:], 1.5, None, ALU.mult)
            nc.gpsimd.tensor_scalar(ident_eps[:], ident[:], EPS, None, ALU.mult)
            nc.gpsimd.memset(cov[:], 0.0)
            nc.gpsimd.memset(halves[:], 0.5).then_inc(ident_ready, 1)
            pool.wait_ge(mask_ready, 1)
            nc.gpsimd.memset(z_sb[:, C, :], 1.0).then_inc(ident_ready, 1)
            pool.wait_ge(ident_ready, 2)

            def split_ty(i, cc, ahead):
                c = channel(i, cc + ahead)
                if not known(i, c):
                    return
                k = (cc + ahead) % 2
                wait(pool, flipped, c + 1)
                nc.gpsimd.tensor_tensor(ty_lo[k][:], hankel[k][:, 1, ::-1], ty_hi[k][:].bitcast(F32),
                                        ALU.subtract).then_inc(ty_lo_done, 1)

            def mask_y(i, cc, behind):
                c = channel(i, cc - behind)
                if not known(i, c):
                    return
                k = (cc - behind) % 2
                wait(pool, y_done, PAIRS * (c + 1))
                wait(pool, z_done, c - 1)
                nc.gpsimd.tensor_tensor(masked[k][:, :, 0:S], y_sb[k].rearrange("p (i w) -> p i w", w=S),
                                        mask[:].rearrange("p (i w) -> p i w", w=S),
                                        ALU.mult).then_inc(masked_done, 1)

            split_ty(0, 0, 0)

            def step(i, cc):
                split_ty(i, cc, 1)
                mask_y(i, cc, 1)

            channels(pool, step)
            mask_y(C // UNROLL - 1, UNROLL, 1)

        @block.scalar
        def _(act):
            for layer in range(3):
                act.wait_ge(f_dve, layer + 1)
                nc.scalar.activation(hid[:], arg[:], ACT.Sin).then_inc(f_sin, 1)
            act.wait_ge(f_dve, 4)
            nc.scalar.activation(decay[:], pos[:], ACT.Exp, scale=rate[:]).then_inc(decay_ready, 1)

            def flip(i, cc, ahead):
                c = channel(i, cc + ahead)
                if not known(i, c):
                    return
                k = (cc + ahead) % 2
                act.wait_ge(hankel_loaded[k], 16 * (c // 2 + 1) if isinstance(c, int)
                            else 16 * (i * (UNROLL // 2) + (cc + ahead) // 2 + 1))
                wait(act, v_mm, PAIRS * (c - 1))
                nc.scalar.copy(tx[k][:], hankel[k][:, 0, ::-1])
                wait(act, y_mm, PAIRS * (c - 1))
                wait(act, ty_lo_done, c - 1)
                nc.scalar.copy(ty_hi[k][:], hankel[k][:, 1, ::-1]).then_inc(flipped, 1)

            def round_v(i, cc, pair):
                q = channel(i, cc) * PAIRS + pair
                wait(act, v_mm, q + 1)
                wait(act, y_mm, q - 1)
                nc.scalar.copy(v_hi[pair][:], ps_v[pair].rearrange("p a n -> p (a n)")).then_inc(v_hi_done, 1)

            flip(0, 0, 0)

            def step(i, cc):
                round_v(i, cc, 0)
                flip(i, cc, 1)
                round_v(i, cc, 1)

            channels(act, step)

            act.wait_ge(n_mm, 1)
            nc.scalar.activation(small[:, 1:2], ps[:, 1, 0:1], ACT.Sqrt).then_inc(n_act, 1)
            act.wait_ge(n_act, 1)
            nc.scalar.activation(small[:, 3:4], small[:, 1:2], ACT.Sqrt).then_inc(n_act, 1)
            act.wait_ge(d_ready, 1)

            def tile(t, k):
                for u in (0, 2):
                    act.wait_ge(t_mm[u], t + 1)
                    if u == 0:
                        wait(act, t_stored[k % O_SLOTS], stored_before(t, k))
                    src = ps[:, 2 * u:2 * u + 2, :].rearrange("p r (h w) -> p r h w", h=HB)
                    dst = t_out[k % O_SLOTS].rearrange("p (h r w) -> p r h w", h=HB, r=TROWS)[:, 2 * u:2 * u + 2]
                    nc.scalar.activation(dst, src, ACT.Identity, bias=small[:, 6:7]).then_inc(t_act, 1)

            tile_loop(act, tile)

        @block.vector
        def _(dve):
            step_sem = ctx.enter_context(nc.semaphore("dve_step"))
            n_step = [0]

            def chained(ins):
                n_step[0] += 1
                ins.then_inc(step_sem, 1)
                dve.wait_ge(step_sem, n_step[0])

            dve.wait_ge(params_loaded, 16 * 13)
            for layer in range(3):
                dve.wait_ge(f_mm, layer + 1)
                chained(nc.vector.tensor_scalar(arg[:], ps[:, 0, 0:S], col[:, layer:layer + 1], col[:, 3:4],
                                                ALU.add, ALU.mult))
                chained(nc.vector.tensor_scalar(turns[:], arg[:], 1.0 / TWO_PI, MAGIC, ALU.mult, ALU.add))
                chained(nc.vector.tensor_scalar(turns[:], turns[:], MAGIC, None, ALU.subtract))
                for part in (PI_HI, PI_MID, PI_LO):
                    chained(nc.vector.scalar_tensor_tensor(arg[:], turns[:], -part, arg[:], ALU.mult, ALU.add))
                nc.vector.tensor_scalar(arg[:], arg[:], PI_BELOW, -PI_BELOW, ALU.min, ALU.max).then_inc(f_dve, 1)
                dve.wait_ge(f_sin, layer + 1)
            dve.wait_ge(pos_ready, 1)
            step = (MAX_DEC - MIN_DEC) / (C - 1)
            chained(nc.vector.tensor_scalar(rate[0:C, :], chan[0:C, :], -step, -MIN_DEC, ALU.mult, ALU.add))
            chained(nc.vector.tensor_scalar(rate[C:P, :], chan[C:P, :], -step, C * step - MIN_DEC, ALU.mult, ALU.add))
            nc.vector.tensor_scalar(rate[:], rate[:], 1.0 / (S - 1), None, ALU.mult).then_inc(f_dve, 1)
            dve.wait_ge(decay_ready, 1)
            chained(nc.vector.tensor_scalar(decay[0:C, :], decay[0:C, :], 1.0 / (2 * S), None, ALU.mult))
            dve.wait_ge(f_mm, 4)
            nc.vector.tensor_tensor(filt[:, 0:S], ps[:, 0, 0:S], decay[:], ALU.mult).then_inc(filt_ready, 1)

            def split_v(i, cc, pair):
                q = channel(i, cc) * PAIRS + pair
                wait(dve, v_hi_done, q + 1)
                nc.vector.tensor_tensor(v_lo[pair][:], ps_v[pair].rearrange("p a n -> p (a n)"),
                                        v_hi[pair][:].bitcast(F32), ALU.subtract).then_inc(v_lo_done, 1)

            def finish_y(i, cc, pair):
                c = channel(i, cc)
                if not known(i, c):
                    return
                q = c * PAIRS + pair
                if pair == 0:
                    stored = 16 * (c // 2) if isinstance(c, int) else 16 * (i * (UNROLL // 2) + cc // 2)
                    wait(dve, y_stored[cc % 2], stored)
                    wait(dve, masked_done, c - 1)
                wait(dve, y_mm, q + 1)
                half = slice(pair * 2 * IMG, (pair + 1) * 2 * IMG)
                nc.vector.scalar_tensor_tensor(y_sb[cc % 2][:, half], x_sb[cc % X_SLOTS][:, half],
                                               bias_sb[:, bass.ds(c, 1)],
                                               ps_y[pair].rearrange("p a n -> p (a n)"),
                                               ALU.mult, ALU.add).then_inc(y_done, 1)

            def sum_masked(i, cc, behind):
                c = channel(i, cc - behind)
                if not known(i, c):
                    return
                wait(dve, masked_done, c + 1)
                nc.vector.tensor_reduce(z_sb[:, bass.ds(c, 1), :].rearrange("p o s -> p (o s)"),
                                        masked[(cc - behind) % 2].rearrange("p i (j u) -> p (i j) u", u=STRIDE),
                                        AX_X, ALU.add).then_inc(z_done, 1)

            def step(i, cc):
                split_v(i, cc, 0)
                finish_y(i, cc - 1, 1)
                sum_masked(i, cc, 2)
                split_v(i, cc, 1)
                finish_y(i, cc, 0)

            channels(dve, step)
            last = C // UNROLL - 1
            finish_y(last, UNROLL - 1, 1)
            sum_masked(last, UNROLL, 2)
            sum_masked(last, UNROLL + 1, 2)

            dve.wait_ge(cov_mm, 1)
            for k in range(2):
                h = slice(k * C, (k + 1) * C)
                chained(nc.vector.scalar_tensor_tensor(cov[h, h], ps[h, 0, 0:C], 1.0 / N_SAMPLES,
                                                       ident_eps[h, h], ALU.mult, ALU.add))
            nc.vector.tensor_scalar(small[:, 5:6], ps[:, 0, C:C + 1], 1.0 / N_SAMPLES, None, ALU.mult)
            chained(nc.vector.tensor_tensor(sq[:], cov[:], cov[:], ALU.mult))
            nc.vector.tensor_reduce(small[:, 0:1], sq[:], AX_X, ALU.add).then_inc(n_dve, 1)
            dve.wait_ge(n_act, 1)
            chained(nc.vector.reciprocal(small[:, 2:3], small[:, 1:2]))
            nc.vector.tensor_scalar(ym[0][:], cov[:], small[:, 2:3], None, ALU.mult).then_inc(n_dve, 1)
            dve.wait_ge(n_act, 2)
            chained(nc.vector.reciprocal(small[:, 4:5], small[:, 3:4]))
            n = 1
            for it in range(N_ITER):
                if it == 0:
                    nc.vector.scalar_tensor_tensor(tm[:], ym[0][:], -0.5, ident15[:], ALU.mult, ALU.add
                                                   ).then_inc(n_dve, 1)
                else:
                    n += 1
                    dve.wait_ge(n_mm, n)
                    nc.vector.scalar_tensor_tensor(tm[:], ps[:, 1, 0:P], -0.5, ident15[:], ALU.mult, ALU.add
                                                   ).then_inc(n_dve, 1)
                a = (it + 1) % 2
                if it < N_ITER - 1:
                    n += 1
                    dve.wait_ge(n_mm, n)
                    nc.vector.tensor_copy(ym[a][:], ps[:, 2, 0:P])
                    nc.vector.tensor_copy(zm[a][:], ps[:, 3, 0:P]).then_inc(n_dve, 1)
                else:
                    n += 1
                    dve.wait_ge(n_mm, n)
                    nc.vector.tensor_scalar(dmat[:], ps[:, 3, 0:P], small[:, 4:5], None, ALU.mult).then_inc(n_dve, 1)
            dve.wait_ge(n_mm, n + 1)
            nc.vector.tensor_scalar(small[:, 6:7], ps[:, 1, 0:1], -1.0, None, ALU.mult).then_inc(d_ready, 1)
            dve.wait_ge(d_ready, 1)

            def tile(t, k):
                for u in (1, 3):
                    dve.wait_ge(t_mm[u], t + 1)
                    if u == 1:
                        wait(dve, t_stored[k % O_SLOTS], stored_before(t, k))
                    src = ps[:, 2 * u:2 * u + 2, :].rearrange("p r (h w) -> p r h w", h=HB)
                    dst = t_out[k % O_SLOTS].rearrange("p (h r w) -> p r h w", h=HB, r=TROWS)[:, 2 * u:2 * u + 2]
                    nc.vector.tensor_scalar(dst, src, small[:, 6:7], None, ALU.add).then_inc(t_dve, 1)

            tile_loop(dve, tile)

        @block.tensor
        def _(pe):
            mm = nc.tensor.matmul
            pe.wait_ge(params_loaded, 16 * 13)
            mm(ps[:, 0, 0:S], w1_sb[:], zt_sb[:], start=True, stop=True).then_inc(f_mm, 1)
            for layer, w_sb in enumerate((w2_sb, w3_sb, wo_sb)):
                pe.wait_ge(f_sin, layer + 1)
                mm(ps[:, 0, 0:S], w_sb[:], hid[:], start=True, stop=True).then_inc(f_mm, 1)
            pe.wait_ge(filt_ready, 1)

            def make_v(i, cc, pair):
                c = channel(i, cc)
                if not known(i, c):
                    return
                q = c * PAIRS + pair
                if pair == 0:
                    k = cc % X_SLOTS
                    pe.wait_ge(x_loaded[k], 16 * (c // X_SLOTS + 1) if isinstance(c, int)
                               else 16 * (i + cc // X_SLOTS + 1))
                    wait(pe, flipped, c + 1)
                wait(pe, v_lo_done, q - 1)
                xs = x_sb[cc % X_SLOTS].rearrange("p (b h w) -> p b h w", b=B, h=HB)
                for im in range(2):
                    for m in range(HB):
                        cols = slice(m * P, (m + 1) * P)
                        for kb in range(HB):
                            last = mm(ps_v[pair][:, im, m * S + kb * P:(m + 1) * S],
                                      xs[:, pair * 2 + im, kb, cols], tx[cc % 2][:, 0:S - kb * P],
                                      start=(kb == 0), stop=(kb == HB - 1))
                last.then_inc(v_mm, 1)

            def make_y(i, cc, pair):
                q = channel(i, cc) * PAIRS + pair
                wait(pe, v_lo_done, q + 1)
                if pair == 0:
                    wait(pe, ty_lo_done, channel(i, cc) + 1)
                wait(pe, y_done, q - 1)
                hi = v_hi[pair][:].rearrange("p (a m h) -> p a m h", a=2, m=HB)
                lo = v_lo[pair][:].rearrange("p (a m h) -> p a m h", a=2, m=HB)
                t_hi, t_lo = ty_hi[cc % 2], ty_lo[cc % 2]
                for im in range(2):
                    for m in range(HB):
                        rows = slice(m * P, (m + 1) * P)
                        for kb in range(HB):
                            o = ps_y[pair][:, im, m * S + kb * P:(m + 1) * S]
                            w = slice(0, S - kb * P)
                            mm(o, hi[:, im, kb, rows], t_hi[:, w], start=(kb == 0), stop=False)
                            mm(o, hi[:, im, kb, rows], t_lo[:, w], start=False, stop=False)
                            last = mm(o, lo[:, im, kb, rows], t_hi[:, w], start=False, stop=(kb == HB - 1))
                last.then_inc(y_mm, 1)

            make_v(0, 0, 0)

            def step(i, cc):
                make_v(i, cc, 1)
                make_y(i, cc, 0)
                make_v(i, cc + 1, 0)
                make_y(i, cc, 1)

            channels(pe, step)

            pe.wait_ge(z_done, C)
            pe.wait_ge(ident_ready, 2)
            pe.wait_ge(v_lo_done, PAIRS * C)
            slots = B * HB * GROUPS
            for s in range(slots):
                for k in range(2):
                    last = mm(ps[k * C:(k + 1) * C, 0, 0:C + 1], z_sb[:, 0:C, s], z_sb[:, :, s],
                              start=(s == 0), stop=(s == slots - 1))
            last.then_inc(cov_mm, 1)
            pe.wait_ge(n_dve, 1)
            mm(ps[:, 1, 0:1], halves[:], small[:, 0:1], start=True, stop=True).then_inc(n_mm, 1)
            n = 2
            for it in range(N_ITER):
                a = it % 2
                zz = ident if it == 0 else zm[a]
                if it > 0:
                    n += 1
                    pe.wait_ge(n_dve, n)
                    mm(ps[:, 1, 0:P], zz[:], ym[a][:], start=True, stop=True).then_inc(n_mm, 1)
                n += 1
                pe.wait_ge(n_dve, n)
                if it < N_ITER - 1:
                    mm(ps[:, 2, 0:P], ym[a][:], tm[:], start=True, stop=True)
                mm(ps[:, 3, 0:P], tm[:], zz[:], start=True, stop=True).then_inc(n_mm, 1)
            pe.wait_ge(n_dve, n + 1)
            mm(ps[:, 1, 0:1], dmat[:], small[:, 5:6], start=True, stop=True).then_inc(n_mm, 1)
            pe.wait_ge(d_ready, 1)

            def tile(t, k):
                pe.wait_ge(t_loaded[k], (t - k) * (32 // T_SLOTS) + 32)
                for u in range(4):
                    wait(pe, t_dve if u % 2 else t_act, 2 * (t - 1) + 1 + u // 2 if not (isinstance(t, int) and t == 0) else 0)
                    for r in range(2):
                        row = 2 * u + r
                        last = mm(ps[:, row, :], dmat[:], t_in[k][:, row * IMG:(row + 1) * IMG],
                                  start=True, stop=True)
                    last.then_inc(t_mm[u], 1)

            tile_loop(pe, tile)


def kernel(**inputs):
    import numpy as np
    import concourse.bacc as bacc
    from concourse.bass_utils import run_bass_kernel_spmd

    a = {k: np.asarray(v) for k, v in inputs.items()}
    x = a["x"].reshape(B, C, HB, P, S).transpose(1, 3, 0, 2, 4).reshape(C, P, B * IMG)

    def both(name, axis):
        pair = [a[f"L0_conv_{n}{name}"] for n in "XY"]
        return np.concatenate([v.reshape(-1, 1) if v.size == ORDER else v for v in pair], axis=axis)

    arrays = {
        "x": x,
        "zt": a["L0_conv_z"][0, ::-1, :].T,
        "w1": both("w1", 1), "b1": both("b1", 0), "w2": both("w2", 0), "b2": both("b2", 0),
        "w3": both("w3", 0), "b3": both("b3", 0), "wo": both("wo", 0), "freq": both("freq", 0),
        "bias": a["L0_conv_bias"].reshape(1, C),
    }
    arrays = {k: np.ascontiguousarray(v) for k, v in arrays.items()}
    nc = bacc.Bacc("TRN2", target_bir_lowering=False, num_devices=1)
    aps = [nc.dram_tensor(k, v.shape, mybir.dt.from_np(v.dtype), kind="ExternalInput").ap()
           for k, v in arrays.items()]
    out = nc.dram_tensor("out", [B, C, S, S], F32, kind="ExternalOutput").ap()
    conv_whiten(nc, *aps, out)
    r = run_bass_kernel_spmd(nc, [arrays], core_ids=[0])
    return r.results[0]["out"]
```

```python
import math
from contextlib import ExitStack

import concourse.bass as bass
from concourse import mybir

F32 = mybir.dt.float32
F32R = mybir.dt.float32r
I32 = mybir.dt.int32
ALU = mybir.AluOpType
ACT = mybir.ActivationFunctionType
AX_X = mybir.AxisListType.X

P = 128
B, C, S = 4, 64, 256
EMB, ORDER = 33, 64
HB = S // P
IMG = HB * S
STRIDE = 9
GROUPS = -(-S // STRIDE)
N_SAMPLES = -(-(B * S * S) // STRIDE)
EPS = 0.01
N_ITER = 5
PAIRS = B // 2
GLEN = S + P
MAGIC = 1.5 * 2.0 ** 23
TWO_PI = 2 * math.pi
PI_HI = 6.28125
PI_MID = math.floor((TWO_PI - PI_HI) * 2.0 ** 21) / 2.0 ** 21
PI_LO = TWO_PI - PI_HI - PI_MID
PI_BELOW = 3.1415925
MIN_DEC = -math.log(0.01) / 1.5
MAX_DEC = -math.log(0.01) / 0.3

UNROLL = 4
X_SLOTS = 4
TROWS = 8
TILES = PAIRS * (P // TROWS)
T_SLOTS = 4
O_SLOTS = 2
UNITS = TROWS // 2


def conv_whiten(nc, x, zt, w1, b1, w2, b2, w3, b3, wo, freq, bias, out):
    g_dram = nc.dram_tensor("filters", [2 * C, GLEN], F32, kind="Internal").ap()
    y_dram = nc.dram_tensor("convolved", [C, P, B * IMG], F32, kind="Internal").ap()

    with ExitStack() as ctx:
        def sb(name, shape, dt=F32):
            return ctx.enter_context(nc.sbuf_tensor(name, shape, dt))

        def sem(name):
            return ctx.enter_context(nc.semaphore(name))

        XW, YW, PW = B * IMG, B * IMG, B * HB * GROUPS * STRIDE
        z_cols = (C + 1) * B * HB * GROUPS
        arena_cols = X_SLOTS * XW + 2 * YW + 2 * PW + z_cols
        arena = sb("arena", [P, arena_cols])
        at = 0
        x_sb = [arena[:, at + k * XW:at + (k + 1) * XW] for k in range(X_SLOTS)]
        at += X_SLOTS * XW
        y_sb = [arena[:, at + k * YW:at + (k + 1) * YW] for k in range(2)]
        at += 2 * YW
        masked = [arena[:, at + k * PW:at + (k + 1) * PW].rearrange("p (i w) -> p i w", i=B * HB)
                  for k in range(2)]
        at += 2 * PW
        z_sb = arena[:, at:at + z_cols].rearrange("p (c s) -> p c s", c=C + 1)
        mask_scratch = [arena[:, at + k * YW:at + (k + 1) * YW] for k in range(3)]
        TW = TROWS * IMG
        t_in = [arena[:, k * TW:(k + 1) * TW] for k in range(T_SLOTS)]
        assert T_SLOTS * TW <= at and O_SLOTS * TW <= z_cols
        t_out = [arena[:, at + k * TW:at + (k + 1) * TW] for k in range(O_SLOTS)]

        mask = sb("mask", [P, B * HB * S])
        hankel = [sb(f"hankel{k}", [P, 2, S]) for k in range(2)]
        t_hi = [sb(f"t_hi{k}", [P, 2, S], F32R) for k in range(2)]
        t_lo = [sb(f"t_lo{k}", [P, 2, S], F32R) for k in range(2)]
        t_f32 = [sb(f"t_f32{k}", [P, 2, P]) for k in range(2)]
        x_hi = [sb(f"x_hi{k}", [P, B, S], F32R) for k in range(2)]
        x_lo = [sb(f"x_lo{k}", [P, B, S], F32R) for k in range(2)]
        v_hi = [sb(f"v_hi{k}", [P, 2, S], F32R) for k in range(2)]
        v_lo = [sb(f"v_lo{k}", [P, 2, S], F32R) for k in range(2)]
        v_f32 = [sb(f"v_f32{k}", [P, 2, S]) for k in range(2)]
        bias_sb = sb("bias_sb", [P, C])
        zt_sb = sb("zt_sb", [EMB, S])
        w1_sb = sb("w1_sb", [EMB, 2 * ORDER])
        w2_sb, w3_sb, wo_sb = (sb(n, [P, P]) for n in ("w2_sb", "w3_sb", "wo_sb"))
        col = sb("col", [P, 4])
        arg, turns, hid = sb("arg", [P, S]), sb("turns", [P, S]), sb("hid", [P, S])
        pos_i, pos, decay = sb("pos_i", [P, S], I32), sb("pos", [P, S]), sb("decay", [P, S])
        chan_i, chan = sb("chan_i", [P, 1], I32), sb("chan", [P, 1])
        rate = sb("rate", [P, 1])
        filt = sb("filt", [P, GLEN])
        ident, ident15, ident_eps = (sb(n, [P, P]) for n in ("ident", "ident15", "ident_eps"))
        halves, twice, sums = sb("halves", [P, P]), sb("twice", [P, P]), sb("sums", [P, C + 1])
        cov, sq = sb("cov", [P, P]), sb("sq", [P, P])
        ym = [sb(f"ym{k}", [P, P]) for k in range(2)]
        zm = [sb(f"zm{k}", [P, P]) for k in range(2)]
        tm = sb("tm", [P, P])
        dmat = sb("dmat", [P, P])
        small = sb("small", [P, 8])

        ps = ctx.enter_context(nc.psum_tensor("ps", [P, 8, S * 2], F32))
        ps_v = [ps[:, 2 * k:2 * k + 2, :] for k in range(2)]
        ps_y = [ps[:, 4 + 2 * k:6 + 2 * k, :] for k in range(2)]

        params_loaded, w_zeroed = sem("params_loaded"), sem("w_zeroed")
        pool_step, ident_ready, mask_ready = sem("pool_step"), sem("ident_ready"), sem("mask_ready")
        pos_ready, f_mm, f_dve, f_sin = sem("pos_ready"), sem("f_mm"), sem("f_dve"), sem("f_sin")
        decay_ready, filt_ready, filt_stored = sem("decay_ready"), sem("filt_ready"), sem("filt_stored")
        x_loaded = [sem(f"x_loaded{k}") for k in range(X_SLOTS)]
        hankel_loaded = [sem(f"hankel_loaded{k}") for k in range(2)]
        flipped, t_lo_done = sem("flipped"), sem("t_lo_done")
        x_hi_done, x_lo_done = sem("x_hi_done"), sem("x_lo_done")
        v_mm, v_hi_done, v_lo_done = sem("v_mm"), sem("v_hi_done"), sem("v_lo_done")
        y_mm, y_done, masked_done, z_done = sem("y_mm"), sem("y_done"), sem("masked_done"), sem("z_done")
        y_stored = [sem(f"y_stored{k}") for k in range(2)]
        cov_mm, n_mm, n_dve, n_act = sem("cov_mm"), sem("n_mm"), sem("n_dve"), sem("n_act")
        sums_ready, d_ready = sem("sums_ready"), sem("d_ready")
        t_loaded = [sem(f"t_loaded{k}") for k in range(T_SLOTS)]
        t_mm = [sem(f"t_mm{u}") for u in range(UNITS)]
        t_act, t_dve = sem("t_act"), sem("t_dve")
        t_stored = [sem(f"t_stored{k}") for k in range(O_SLOTS)]

        def channels(eng, step):
            n = C // UNROLL
            for cc in range(UNROLL):
                step(0, cc)
            with eng.Fori(1, n - 1) as i:
                for cc in range(UNROLL):
                    step(i, cc)
            for cc in range(UNROLL):
                step(n - 1, cc)

        def wait(eng, s, value):
            if not isinstance(value, int) or value > 0:
                eng.wait_ge(s, value)

        def channel(i, cc):
            return i * UNROLL + cc

        def known(i, c):
            return not isinstance(i, int) or 0 <= c < C

        def stored_before(t, k):
            return (t - k % O_SLOTS) * (32 // O_SLOTS)

        def tile_loop(eng, step):
            for k in range(T_SLOTS):
                step(k, k)
            with eng.Fori(1, TILES // T_SLOTS - 1) as j:
                for k in range(T_SLOTS):
                    step(j * T_SLOTS + k, k)
            for k in range(T_SLOTS):
                step(TILES - T_SLOTS + k, k)

        def row_block_0(slot):
            return x_sb[slot].rearrange("p (b h w) -> p b h w", b=B, h=HB)[:, :, 0, :]

        block = ctx.enter_context(nc.Block())

        @block.sync
        def _(sp):
            sp.dma_start(zt_sb[:], zt).then_inc(params_loaded, 16)
            sp.dma_start(w1_sb[:], w1).then_inc(params_loaded, 16)
            for j, v in enumerate((b1, b2, b3, freq)):
                sp.dma_start(col[:, j:j + 1], v).then_inc(params_loaded, 16)
            sp.dma_start(bias_sb[:], bias.to_broadcast([P, C])).then_inc(params_loaded, 16)
            sp.wait_ge(w_zeroed, 3)
            for w_sb, w in ((w2_sb, w2), (w3_sb, w3), (wo_sb, wo)):
                for k in range(2):
                    h = slice(k * ORDER, (k + 1) * ORDER)
                    sp.dma_start(w_sb[h, h], w[h, :]).then_inc(params_loaded, 16)

            def load_x(i, cc, ahead):
                c = channel(i, cc + ahead)
                if not known(i, c):
                    return
                wait(sp, y_done, PAIRS * (c - X_SLOTS) + PAIRS)
                sp.dma_start(x_sb[(cc + ahead) % X_SLOTS], x[bass.ds(c, 1), :, :].rearrange("o p n -> (o p) n")).then_inc(
                    x_loaded[(cc + ahead) % X_SLOTS], 16)

            def load_hankel(i, cc, ahead):
                c = channel(i, cc + ahead)
                if not known(i, c):
                    return
                k = (cc + ahead) % 2
                wait(sp, flipped, c - 1)
                wait(sp, t_lo_done, c - 1)
                src = bass.AP(tensor=g_dram.tensor, offset=c * GLEN, ap=[[1, P], [C * GLEN, 2], [1, S]])
                sp.dma_start(hankel[k][:], src).then_inc(hankel_loaded[k], 16)

            def store_y(i, cc, behind):
                c = channel(i, cc - behind)
                if not known(i, c):
                    return
                k = (cc - behind) % 2
                wait(sp, y_done, PAIRS * (c + 1))
                sp.dma_start(y_dram[bass.ds(c, 1), :, :].rearrange("o p n -> (o p) n"), y_sb[k]).then_inc(y_stored[k], 16)

            for c in range(X_SLOTS - 1):
                load_x(0, 0, c)
            sp.wait_ge(filt_ready, 1)
            sp.dma_start(g_dram, filt[:]).then_inc(filt_stored, 16)
            sp.wait_ge(filt_stored, 16)
            load_hankel(0, 0, 0)
            load_hankel(0, 0, 1)

            def step(i, cc):
                load_hankel(i, cc, 2)
                load_x(i, cc, X_SLOTS - 1)
                store_y(i, cc, 1)

            channels(sp, step)
            store_y(C // UNROLL - 1, UNROLL, 1)

            for k in range(2):
                sp.wait_ge(y_stored[k], 16 * (C // 2))
            sp.wait_ge(z_done, C)
            sp.wait_ge(y_done, PAIRS * C)

            def load_tile(t, k):
                for b in range(2):
                    src = bass.AP(tensor=y_dram.tensor,
                                  offset=(t - k % PAIRS) * (TROWS * B * IMG // PAIRS) + (k % PAIRS * 2 + b) * IMG,
                                  ap=[[P * B * IMG, C], [B * IMG, TROWS], [1, IMG]])
                    sp.dma_start(t_in[k][b * C:(b + 1) * C, :].rearrange("c (r n) -> c r n", r=TROWS),
                                 src).then_inc(t_loaded[k], 16)

            def store_tile(t, k):
                for b in range(2):
                    dst = bass.AP(tensor=out.tensor,
                                  offset=(t - k % PAIRS) * (TROWS * S // PAIRS) + (k % PAIRS * 2 + b) * C * S * S,
                                  ap=[[S * S, C], [P * S, HB], [1, TROWS * S]])
                    sp.dma_start(dst, t_out[k % O_SLOTS][b * C:(b + 1) * C, :].rearrange(
                        "c (h n) -> c h n", h=HB)).then_inc(t_stored[k % O_SLOTS], 16)

            ahead = T_SLOTS - 1

            def tile(t, k):
                if not isinstance(t, int) or t + ahead < TILES:
                    wait(sp, t_mm[UNITS - 1], t)
                    load_tile(t + ahead, (k + ahead) % T_SLOTS)
                sp.wait_ge(t_act, 2 * t + 2)
                sp.wait_ge(t_dve, 2 * t + 2)
                store_tile(t, k)

            for k in range(ahead):
                load_tile(k, k)
            tile_loop(sp, tile)
            for k in range(O_SLOTS):
                sp.wait_ge(t_stored[k], 32 * (TILES // O_SLOTS))

        @block.gpsimd
        def _(pool):
            n_step = [0]

            def chained(ins):
                n_step[0] += 1
                ins.then_inc(pool_step, 1)
                pool.wait_ge(pool_step, n_step[0])

            for w_sb in (w2_sb, w3_sb, wo_sb):
                nc.gpsimd.memset(w_sb[:], 0.0).then_inc(w_zeroed, 1)
            nc.gpsimd.memset(filt[:], 0.0)
            nc.gpsimd.iota(pos_i[:], pattern=[[-1, S]], base=S - 1, channel_multiplier=0)
            chained(nc.gpsimd.iota(chan_i[:], pattern=[[0, 1]], base=0, channel_multiplier=1))
            nc.gpsimd.tensor_copy(pos[:], pos_i[:])
            nc.gpsimd.tensor_copy(chan[:], chan_i[:]).then_inc(pos_ready, 1)
            idx_i, idx, near = mask_scratch[0].bitcast(I32), mask_scratch[1], mask_scratch[2]
            chained(nc.gpsimd.iota(idx_i.rearrange("p (b h w) -> p b h w", b=B, h=HB),
                                   pattern=[[(S * S) % STRIDE, B], [(S * P) % STRIDE, HB], [1, S]],
                                   base=0, channel_multiplier=S % STRIDE))
            chained(nc.gpsimd.tensor_copy(idx, idx_i))
            chained(nc.gpsimd.tensor_scalar(near, idx, 1.0 / STRIDE, MAGIC, ALU.mult, ALU.add))
            chained(nc.gpsimd.tensor_scalar(near, near, MAGIC, float(STRIDE), ALU.subtract, ALU.mult))
            chained(nc.gpsimd.tensor_tensor(idx, idx, near, ALU.subtract))
            nc.gpsimd.tensor_scalar(mask[:], idx, 0.0, None, ALU.is_equal).then_inc(mask_ready, 1)
            for k in range(2):
                nc.gpsimd.memset(masked[k][:, :, S:], 0.0)
            chained(nc.gpsimd.memset(ident[:], 0.0))
            chained(nc.gpsimd.affine_select(out=ident[:], in_=ident[:], compare_op=ALU.not_equal, fill=1.0,
                                            base=0, pattern=[[-1, P]], channel_multiplier=1))
            nc.gpsimd.tensor_scalar(ident15[:], ident[:], 1.5, None, ALU.mult)
            nc.gpsimd.tensor_scalar(ident_eps[:], ident[:], EPS, None, ALU.mult)
            for k in range(2):
                nc.gpsimd.tensor_copy(twice[0:C, k * C:(k + 1) * C], ident[0:C, 0:C])
            nc.gpsimd.memset(cov[:], 0.0)
            nc.gpsimd.memset(halves[:], 0.5).then_inc(ident_ready, 1)
            pool.wait_ge(mask_ready, 1)
            nc.gpsimd.memset(z_sb[:, C, :], 1.0).then_inc(ident_ready, 1)
            pool.wait_ge(ident_ready, 2)

            def split_x(i, cc, ahead):
                c = channel(i, cc + ahead)
                if not known(i, c):
                    return
                k = (cc + ahead) % 2
                wait(pool, x_hi_done, c + 1)
                nc.gpsimd.tensor_tensor(x_lo[k][:], row_block_0((cc + ahead) % X_SLOTS),
                                        x_hi[k][:].bitcast(F32), ALU.subtract).then_inc(x_lo_done, 1)

            def mask_y(i, cc, behind):
                c = channel(i, cc - behind)
                if not known(i, c):
                    return
                k = (cc - behind) % 2
                wait(pool, y_done, PAIRS * (c + 1))
                wait(pool, z_done, c - 1)
                nc.gpsimd.tensor_tensor(masked[k][:, :, 0:S], y_sb[k].rearrange("p (i w) -> p i w", w=S),
                                        mask[:].rearrange("p (i w) -> p i w", w=S),
                                        ALU.mult).then_inc(masked_done, 1)

            split_x(0, 0, 0)

            def step(i, cc):
                split_x(i, cc, 1)
                mask_y(i, cc, 1)

            channels(pool, step)
            mask_y(C // UNROLL - 1, UNROLL, 1)

        @block.scalar
        def _(act):
            for layer in range(3):
                act.wait_ge(f_dve, layer + 1)
                nc.scalar.activation(hid[:], arg[:], ACT.Sin).then_inc(f_sin, 1)
            act.wait_ge(f_dve, 4)
            nc.scalar.activation(decay[:], pos[:], ACT.Exp, scale=rate[:]).then_inc(decay_ready, 1)

            def flip(i, cc, ahead):
                c = channel(i, cc + ahead)
                if not known(i, c):
                    return
                k = (cc + ahead) % 2
                act.wait_ge(hankel_loaded[k], 16 * (c // 2 + 1) if isinstance(c, int)
                            else 16 * (i * (UNROLL // 2) + (cc + ahead) // 2 + 1))
                wait(act, y_mm, PAIRS * (c - 1))
                wait(act, t_lo_done, c - 1)
                nc.scalar.copy(t_f32[k][:], hankel[k][:, :, :P - 1:-1])
                nc.scalar.copy(t_hi[k][:], hankel[k][:, :, ::-1]).then_inc(flipped, 1)

            def round_x(i, cc, ahead):
                c = channel(i, cc + ahead)
                if not known(i, c):
                    return
                k = (cc + ahead) % X_SLOTS
                act.wait_ge(x_loaded[k], 16 * (c // X_SLOTS + 1) if isinstance(c, int)
                            else 16 * (i + (cc + ahead) // X_SLOTS + 1))
                wait(act, v_mm, PAIRS * (c - 1))
                nc.scalar.copy(x_hi[(cc + ahead) % 2][:], row_block_0(k)).then_inc(x_hi_done, 1)

            def round_v(i, cc, pair):
                q = channel(i, cc) * PAIRS + pair
                wait(act, v_mm, q + 1)
                wait(act, y_mm, q - 1)
                nc.scalar.copy(v_f32[pair][:], ps_v[pair][:, :, S:2 * S])
                nc.scalar.copy(v_hi[pair][:], ps_v[pair][:, :, 0:S]).then_inc(v_hi_done, 1)

            round_x(0, 0, 0)
            flip(0, 0, 0)

            def step(i, cc):
                round_x(i, cc, 1)
                round_v(i, cc, 0)
                flip(i, cc, 1)
                round_v(i, cc, 1)

            channels(act, step)

            act.wait_ge(n_mm, 1)
            nc.scalar.activation(small[:, 1:2], ps[:, 0, 0:1], ACT.Sqrt).then_inc(n_act, 1)
            act.wait_ge(n_act, 1)
            nc.scalar.activation(small[:, 3:4], small[:, 1:2], ACT.Sqrt).then_inc(n_act, 1)
            act.wait_ge(d_ready, 1)

            def tile(t, k):
                for u in (0, 2):
                    act.wait_ge(t_mm[u], t + 1)
                    if u == 0:
                        wait(act, t_stored[k % O_SLOTS], stored_before(t, k))
                    src = ps[:, 2 * u:2 * u + 2, :].rearrange("p r (h w) -> p r h w", h=HB)
                    dst = t_out[k % O_SLOTS].rearrange("p (h r w) -> p r h w", h=HB, r=TROWS)[:, 2 * u:2 * u + 2]
                    nc.scalar.activation(dst, src, ACT.Identity, bias=small[:, 6:7]).then_inc(t_act, 1)

            tile_loop(act, tile)

        @block.vector
        def _(dve):
            step_sem = ctx.enter_context(nc.semaphore("dve_step"))
            n_step = [0]

            def chained(ins):
                n_step[0] += 1
                ins.then_inc(step_sem, 1)
                dve.wait_ge(step_sem, n_step[0])

            dve.wait_ge(params_loaded, 16 * 13)
            for layer in range(3):
                dve.wait_ge(f_mm, layer + 1)
                chained(nc.vector.tensor_scalar(arg[:], ps[:, 0, 0:S], col[:, layer:layer + 1], col[:, 3:4],
                                                ALU.add, ALU.mult))
                chained(nc.vector.tensor_scalar(turns[:], arg[:], 1.0 / TWO_PI, MAGIC, ALU.mult, ALU.add))
                chained(nc.vector.tensor_scalar(turns[:], turns[:], MAGIC, None, ALU.subtract))
                for part in (PI_HI, PI_MID, PI_LO):
                    chained(nc.vector.scalar_tensor_tensor(arg[:], turns[:], -part, arg[:], ALU.mult, ALU.add))
                nc.vector.tensor_scalar(arg[:], arg[:], PI_BELOW, -PI_BELOW, ALU.min, ALU.max).then_inc(f_dve, 1)
                dve.wait_ge(f_sin, layer + 1)
            dve.wait_ge(pos_ready, 1)
            step = (MAX_DEC - MIN_DEC) / (C - 1)
            chained(nc.vector.tensor_scalar(rate[0:C, :], chan[0:C, :], -step, -MIN_DEC, ALU.mult, ALU.add))
            chained(nc.vector.tensor_scalar(rate[C:P, :], chan[C:P, :], -step, C * step - MIN_DEC, ALU.mult, ALU.add))
            nc.vector.tensor_scalar(rate[:], rate[:], 1.0 / (S - 1), None, ALU.mult).then_inc(f_dve, 1)
            dve.wait_ge(decay_ready, 1)
            chained(nc.vector.tensor_scalar(decay[0:C, :], decay[0:C, :], 1.0 / (2 * S), None, ALU.mult))
            dve.wait_ge(f_mm, 4)
            nc.vector.tensor_tensor(filt[:, 0:S], ps[:, 0, 0:S], decay[:], ALU.mult).then_inc(filt_ready, 1)

            def split_v(i, cc, pair):
                q = channel(i, cc) * PAIRS + pair
                wait(dve, v_hi_done, q + 1)
                nc.vector.tensor_tensor(v_lo[pair][:], ps_v[pair][:, :, 0:S],
                                        v_hi[pair][:].bitcast(F32), ALU.subtract).then_inc(v_lo_done, 1)

            def split_t(i, cc, ahead):
                c = channel(i, cc + ahead)
                if not known(i, c):
                    return
                k = (cc + ahead) % 2
                wait(dve, flipped, c + 1)
                nc.vector.tensor_tensor(t_lo[k][:], hankel[k][:, :, ::-1], t_hi[k][:].bitcast(F32),
                                        ALU.subtract).then_inc(t_lo_done, 1)

            def finish_y(i, cc, pair):
                c = channel(i, cc)
                if not known(i, c):
                    return
                q = c * PAIRS + pair
                if pair == 0:
                    stored = 16 * (c // 2) if isinstance(c, int) else 16 * (i * (UNROLL // 2) + cc // 2)
                    wait(dve, y_stored[cc % 2], stored)
                    wait(dve, masked_done, c - 1)
                wait(dve, y_mm, q + 1)
                half = slice(pair * 2 * IMG, (pair + 1) * 2 * IMG)
                nc.vector.scalar_tensor_tensor(y_sb[cc % 2][:, half], x_sb[cc % X_SLOTS][:, half],
                                               bias_sb[:, bass.ds(c, 1)],
                                               ps_y[pair].rearrange("p a n -> p (a n)"),
                                               ALU.mult, ALU.add).then_inc(y_done, 1)

            def sum_masked(i, cc, behind):
                c = channel(i, cc - behind)
                if not known(i, c):
                    return
                wait(dve, masked_done, c + 1)
                nc.vector.tensor_reduce(z_sb[:, bass.ds(c, 1), :].rearrange("p o s -> p (o s)"),
                                        masked[(cc - behind) % 2].rearrange("p i (j u) -> p (i j) u", u=STRIDE),
                                        AX_X, ALU.add).then_inc(z_done, 1)

            split_t(0, 0, 0)

            def step(i, cc):
                split_v(i, cc, 0)
                finish_y(i, cc - 1, 1)
                split_t(i, cc, 1)
                sum_masked(i, cc, 2)
                split_v(i, cc, 1)
                finish_y(i, cc, 0)

            channels(dve, step)
            last = C // UNROLL - 1
            finish_y(last, UNROLL - 1, 1)
            sum_masked(last, UNROLL, 2)
            sum_masked(last, UNROLL + 1, 2)

            dve.wait_ge(cov_mm, 1)
            nc.vector.tensor_copy(sums[0:C, :], ps[0:C, 0, 0:C + 1]).then_inc(sums_ready, 1)
            dve.wait_ge(cov_mm, 2)
            for k in range(2):
                h = slice(k * C, (k + 1) * C)
                chained(nc.vector.scalar_tensor_tensor(cov[h, h], ps[h, 1, 0:C], 1.0 / N_SAMPLES,
                                                       ident_eps[h, h], ALU.mult, ALU.add))
            nc.vector.tensor_scalar(small[:, 5:6], ps[:, 1, C:C + 1], 1.0 / N_SAMPLES, None, ALU.mult)
            chained(nc.vector.tensor_tensor(sq[:], cov[:], cov[:], ALU.mult))
            nc.vector.tensor_reduce(small[:, 0:1], sq[:], AX_X, ALU.add).then_inc(n_dve, 1)
            dve.wait_ge(n_act, 1)
            chained(nc.vector.reciprocal(small[:, 2:3], small[:, 1:2]))
            nc.vector.tensor_scalar(ym[0][:], cov[:], small[:, 2:3], None, ALU.mult).then_inc(n_dve, 1)
            dve.wait_ge(n_act, 2)
            chained(nc.vector.reciprocal(small[:, 4:5], small[:, 3:4]))
            n = 1
            for it in range(N_ITER):
                if it == 0:
                    nc.vector.scalar_tensor_tensor(tm[:], ym[0][:], -0.5, ident15[:], ALU.mult, ALU.add
                                                   ).then_inc(n_dve, 1)
                else:
                    n += 1
                    dve.wait_ge(n_mm, n)
                    nc.vector.scalar_tensor_tensor(tm[:], ps[:, 1, 0:P], -0.5, ident15[:], ALU.mult, ALU.add
                                                   ).then_inc(n_dve, 1)
                a = (it + 1) % 2
                if it < N_ITER - 1:
                    n += 1
                    dve.wait_ge(n_mm, n)
                    nc.vector.tensor_copy(ym[a][:], ps[:, 2, 0:P])
                    nc.vector.tensor_copy(zm[a][:], ps[:, 3, 0:P]).then_inc(n_dve, 1)
                else:
                    n += 1
                    dve.wait_ge(n_mm, n)
                    nc.vector.tensor_scalar(dmat[:], ps[:, 3, 0:P], small[:, 4:5], None, ALU.mult).then_inc(n_dve, 1)
            dve.wait_ge(n_mm, n + 1)
            nc.vector.tensor_scalar(small[:, 6:7], ps[:, 1, 0:1], -1.0, None, ALU.mult).then_inc(d_ready, 1)
            dve.wait_ge(d_ready, 1)

            def tile(t, k):
                for u in (1, 3):
                    dve.wait_ge(t_mm[u], t + 1)
                    if u == 1:
                        wait(dve, t_stored[k % O_SLOTS], stored_before(t, k))
                    src = ps[:, 2 * u:2 * u + 2, :].rearrange("p r (h w) -> p r h w", h=HB)
                    dst = t_out[k % O_SLOTS].rearrange("p (h r w) -> p r h w", h=HB, r=TROWS)[:, 2 * u:2 * u + 2]
                    nc.vector.tensor_scalar(dst, src, small[:, 6:7], None, ALU.add).then_inc(t_dve, 1)

            tile_loop(dve, tile)

        @block.tensor
        def _(pe):
            mm = nc.tensor.matmul
            pe.wait_ge(params_loaded, 16 * 13)
            mm(ps[:, 0, 0:S], w1_sb[:], zt_sb[:], start=True, stop=True).then_inc(f_mm, 1)
            for layer, w_sb in enumerate((w2_sb, w3_sb, wo_sb)):
                pe.wait_ge(f_sin, layer + 1)
                mm(ps[:, 0, 0:S], w_sb[:], hid[:], start=True, stop=True).then_inc(f_mm, 1)
            pe.wait_ge(filt_ready, 1)

            def toeplitz(o, hi, lo, block1, k, f):
                for im in range(2):
                    for m in range(HB):
                        cols = slice(m * P, (m + 1) * P)
                        wide = o[:, im, m * S:(m + 1) * S]
                        mm(wide, hi[:, im, cols], t_hi[k][:, f, :], start=True, stop=False)
                        mm(wide, hi[:, im, cols], t_lo[k][:, f, :], start=False, stop=False)
                        mm(wide, lo[:, im, cols], t_hi[k][:, f, :], start=False, stop=False)
                        last = mm(o[:, im, m * S + P:(m + 1) * S], block1[:, im, cols], t_f32[k][:, f, :],
                                  start=False, stop=True)
                return last

            def make_v(i, cc, pair):
                c = channel(i, cc)
                if not known(i, c):
                    return
                q = c * PAIRS + pair
                if pair == 0:
                    wait(pe, x_lo_done, c + 1)
                    wait(pe, t_lo_done, c + 1)
                wait(pe, v_lo_done, q - 1)
                images = slice(pair * 2, pair * 2 + 2)
                toeplitz(ps_v[pair], x_hi[cc % 2][:, images, :], x_lo[cc % 2][:, images, :],
                         x_sb[cc % X_SLOTS].rearrange("p (b h w) -> p b h w", b=B, h=HB)[:, images, 1, :],
                         cc % 2, 0).then_inc(v_mm, 1)

            def make_y(i, cc, pair):
                q = channel(i, cc) * PAIRS + pair
                wait(pe, v_lo_done, q + 1)
                wait(pe, y_done, q - 1)
                toeplitz(ps_y[pair], v_hi[pair], v_lo[pair], v_f32[pair], cc % 2, 1).then_inc(y_mm, 1)

            make_v(0, 0, 0)

            def step(i, cc):
                make_v(i, cc, 1)
                make_y(i, cc, 0)
                make_v(i, cc + 1, 0)
                make_y(i, cc, 1)

            channels(pe, step)

            pe.wait_ge(z_done, C)
            pe.wait_ge(ident_ready, 2)
            pe.wait_ge(v_lo_done, PAIRS * C)
            slots = B * HB * GROUPS
            for s in range(slots):
                last = mm(ps[0:C, 0, 0:C + 1], z_sb[:, 0:C, s], z_sb[:, :, s],
                          start=(s == 0), stop=(s == slots - 1))
            last.then_inc(cov_mm, 1)
            pe.wait_ge(sums_ready, 1)
            mm(ps[:, 1, 0:C + 1], twice[0:C, :], sums[0:C, :], start=True, stop=True).then_inc(cov_mm, 1)
            pe.wait_ge(n_dve, 1)
            mm(ps[:, 0, 0:1], halves[:], small[:, 0:1], start=True, stop=True).then_inc(n_mm, 1)
            n = 2
            for it in range(N_ITER):
                a = it % 2
                zz = ident if it == 0 else zm[a]
                if it > 0:
                    n += 1
                    pe.wait_ge(n_dve, n)
                    mm(ps[:, 1, 0:P], zz[:], ym[a][:], start=True, stop=True).then_inc(n_mm, 1)
                n += 1
                pe.wait_ge(n_dve, n)
                if it < N_ITER - 1:
                    mm(ps[:, 2, 0:P], ym[a][:], tm[:], start=True, stop=True)
                mm(ps[:, 3, 0:P], tm[:], zz[:], start=True, stop=True).then_inc(n_mm, 1)
            pe.wait_ge(n_dve, n + 1)
            mm(ps[:, 1, 0:1], dmat[:], small[:, 5:6], start=True, stop=True).then_inc(n_mm, 1)
            pe.wait_ge(d_ready, 1)

            def tile(t, k):
                pe.wait_ge(t_loaded[k], (t - k) * (32 // T_SLOTS) + 32)
                for u in range(4):
                    wait(pe, t_dve if u % 2 else t_act, 2 * (t - 1) + 1 + u // 2 if not (isinstance(t, int) and t == 0) else 0)
                    for r in range(2):
                        row = 2 * u + r
                        last = mm(ps[:, row, :], dmat[:], t_in[k][:, row * IMG:(row + 1) * IMG],
                                  start=True, stop=True)
                    last.then_inc(t_mm[u], 1)

            tile_loop(pe, tile)


def kernel(**inputs):
    import numpy as np
    import concourse.bacc as bacc
    from concourse.bass_utils import run_bass_kernel_spmd

    a = {k: np.asarray(v) for k, v in inputs.items()}
    x = a["x"].reshape(B, C, HB, P, S).transpose(1, 3, 0, 2, 4).reshape(C, P, B * IMG)

    def both(name, axis):
        pair = [a[f"L0_conv_{n}{name}"] for n in "XY"]
        return np.concatenate([v.reshape(-1, 1) if v.size == ORDER else v for v in pair], axis=axis)

    arrays = {
        "x": x,
        "zt": a["L0_conv_z"][0, ::-1, :].T,
        "w1": both("w1", 1), "b1": both("b1", 0), "w2": both("w2", 0), "b2": both("b2", 0),
        "w3": both("w3", 0), "b3": both("b3", 0), "wo": both("wo", 0), "freq": both("freq", 0),
        "bias": a["L0_conv_bias"].reshape(1, C),
    }
    arrays = {k: np.ascontiguousarray(v) for k, v in arrays.items()}
    nc = bacc.Bacc("TRN2", target_bir_lowering=False, num_devices=1)
    aps = [nc.dram_tensor(k, v.shape, mybir.dt.from_np(v.dtype), kind="ExternalInput").ap()
           for k, v in arrays.items()]
    out = nc.dram_tensor("out", [B, C, S, S], F32, kind="ExternalOutput").ap()
    conv_whiten(nc, *aps, out)
    r = run_bass_kernel_spmd(nc, [arrays], core_ids=[0])
    return r.results[0]["out"]
```

```python
import math
from contextlib import ExitStack

import concourse.bass as bass
from concourse import mybir

F32 = mybir.dt.float32
F32R = mybir.dt.float32r
I32 = mybir.dt.int32
ALU = mybir.AluOpType
ACT = mybir.ActivationFunctionType
AX_X = mybir.AxisListType.X

P = 128
B, C, S = 4, 64, 256
EMB, ORDER = 33, 64
HB = S // P
IMG = HB * S
STRIDE = 9
GROUPS = -(-S // STRIDE)
N_SAMPLES = -(-(B * S * S) // STRIDE)
EPS = 0.01
N_ITER = 5
PAIRS = B // 2
GLEN = S + P
MAGIC = 1.5 * 2.0 ** 23
TWO_PI = 2 * math.pi
PI_HI = 6.28125
PI_MID = math.floor((TWO_PI - PI_HI) * 2.0 ** 21) / 2.0 ** 21
PI_LO = TWO_PI - PI_HI - PI_MID
PI_BELOW = 3.1415925
MIN_DEC = -math.log(0.01) / 1.5
MAX_DEC = -math.log(0.01) / 0.3

UNROLL = 4
X_SLOTS = 4
TROWS = 4
TILES = PAIRS * (P // TROWS)
T_SLOTS = 16
O_SLOTS = 4
UNITS = 2


def conv_whiten(nc, x, first, hidden, columns, bias, out):
    g_dram = nc.dram_tensor("filters", [2 * C, GLEN], F32, kind="Internal").ap()
    y_dram = nc.dram_tensor("convolved", [C, P, B * IMG], F32, kind="Internal").ap()

    with ExitStack() as ctx:
        def sb(name, shape, dt=F32):
            return ctx.enter_context(nc.sbuf_tensor(name, shape, dt))

        def sem(name):
            return ctx.enter_context(nc.semaphore(name))

        XW, YW, PW = B * IMG, B * IMG, B * HB * GROUPS * STRIDE
        z_cols = (C + 1) * B * HB * GROUPS
        arena_cols = X_SLOTS * XW + 2 * YW + 2 * PW + z_cols
        arena = sb("arena", [P, arena_cols])
        at = 0
        x_sb = [arena[:, at + k * XW:at + (k + 1) * XW] for k in range(X_SLOTS)]
        at += X_SLOTS * XW
        y_sb = [arena[:, at + k * YW:at + (k + 1) * YW] for k in range(2)]
        at += 2 * YW
        masked = [arena[:, at + k * PW:at + (k + 1) * PW].rearrange("p (i w) -> p i w", i=B * HB)
                  for k in range(2)]
        at += 2 * PW
        z_sb = arena[:, at:at + z_cols].rearrange("p (c s) -> p c s", c=C + 1)
        mask_scratch = [arena[:, at + k * YW:at + (k + 1) * YW] for k in range(3)]
        TW = TROWS * IMG
        t_in = [arena[:, k * TW:(k + 1) * TW] for k in range(at // TW)]
        filter_space, block_space, mask = (sb(n, [P, TW]) for n in ("filter_space", "block_space", "mask"))
        t_in += [filter_space[:, :], block_space[:, :], mask[:, :]]
        t_in += [sb(f"t_in_own{k}", [P, TW])[:, :] for k in range(2)]
        early = len(t_in)
        t_out = [arena[:, at + k * TW:at + (k + 1) * TW] for k in range(O_SLOTS)]
        t_in += [arena[:, at + k * TW:at + (k + 1) * TW] for k in range(O_SLOTS, z_cols // TW)]
        assert len(t_in) == T_SLOTS

        assert TW == B * HB * S
        hankel = [block_space[:, k * 2 * S:(k + 1) * 2 * S].rearrange("p (f n) -> p f n", f=2)
                  for k in range(2)]
        t_hi = [sb(f"t_hi{k}", [P, 2, S], F32R) for k in range(2)]
        t_lo = [sb(f"t_lo{k}", [P, 2, S], F32R) for k in range(2)]
        t_f32 = [sb(f"t_f32{k}", [P, 2, P]) for k in range(2)]
        x_hi = [sb(f"x_hi{k}", [P, B, S], F32R) for k in range(2)]
        x_lo = [sb(f"x_lo{k}", [P, B, S], F32R) for k in range(2)]
        v_hi = [sb(f"v_hi{k}", [P, 2, S], F32R) for k in range(2)]
        v_lo = [sb(f"v_lo{k}", [P, 2, S], F32R) for k in range(2)]
        v_f32 = [sb(f"v_f32{k}", [P, 2, S]) for k in range(2)]
        bias_sb = sb("bias_sb", [P, C])
        first_sb = block_space[0:EMB, 4 * S:4 * S + 2 * ORDER + S]
        w_sb = block_space[:, 6 * S:6 * S + 3 * P].rearrange("p (l n) -> p l n", l=3)
        col = sb("col", [P, 4])
        arg, turns, hid, pos_f, pos, decay = (filter_space[:, k * S:(k + 1) * S] for k in range(6))
        pos_i = pos_f.bitcast(I32)
        chan_i, chan = sb("chan_i", [P, 1], I32), sb("chan", [P, 1])
        rate = sb("rate", [P, 1])
        filt = filter_space[:, 6 * S:6 * S + GLEN]
        ident, ident15, ident_eps = (sb(n, [P, P]) for n in ("ident", "ident15", "ident_eps"))
        halves, twice, sums = sb("halves", [P, P]), sb("twice", [P, P]), sb("sums", [P, C + 1])
        cov = sb("cov", [P, P])
        ym = [sb(f"ym{k}", [P, P]) for k in range(2)]
        zm = [sb(f"zm{k}", [P, P]) for k in range(2)]
        rest = at + z_cols // TW * TW
        assert rest + 3 * P <= arena_cols
        sq, tm, dmat = (arena[:, rest + k * P:rest + (k + 1) * P] for k in range(3))
        small = sb("small", [P, 8])

        ps = ctx.enter_context(nc.psum_tensor("ps", [P, 8, S * 2], F32))
        ps_v = [ps[:, 2 * k:2 * k + 2, :] for k in range(2)]
        ps_y = [ps[:, 4 + 2 * k:6 + 2 * k, :] for k in range(2)]

        params_loaded, bias_loaded, w_zeroed = sem("params_loaded"), sem("bias_loaded"), sem("w_zeroed")
        pool_step, ident_ready = sem("pool_step"), sem("ident_ready")
        index_ready, mask_ready = sem("index_ready"), sem("mask_ready")
        pos_ready, f_mm, f_dve, f_sin = sem("pos_ready"), sem("f_mm"), sem("f_dve"), sem("f_sin")
        filt_zeroed, rate_ready = sem("filt_zeroed"), sem("rate_ready")
        decay_ready, filt_ready, filt_stored = sem("decay_ready"), sem("filt_ready"), sem("filt_stored")
        x_loaded = [sem(f"x_loaded{k}") for k in range(X_SLOTS)]
        hankel_loaded = [sem(f"hankel_loaded{k}") for k in range(2)]
        flipped, t_lo_done = sem("flipped"), sem("t_lo_done")
        x_hi_done, x_lo_done = sem("x_hi_done"), sem("x_lo_done")
        v_mm, v_hi_done, v_lo_done = sem("v_mm"), sem("v_hi_done"), sem("v_lo_done")
        y_mm, y_done, masked_done, z_done = sem("y_mm"), sem("y_done"), sem("masked_done"), sem("z_done")
        y_stored = [sem(f"y_stored{k}") for k in range(2)]
        cov_mm, n_mm, n_dve, n_act = sem("cov_mm"), sem("n_mm"), sem("n_dve"), sem("n_act")
        z_last_done = sem("z_last_done")
        sums_ready, d_ready = sem("sums_ready"), sem("d_ready")
        t_loaded = [sem(f"t_loaded{k}") for k in range(T_SLOTS)]
        t_mm = [sem(f"t_mm{u}") for u in range(UNITS)]
        t_act, t_dve = sem("t_act"), sem("t_dve")
        t_stored = [sem(f"t_stored{k}") for k in range(O_SLOTS)]

        def channels(eng, step):
            n = C // UNROLL
            for cc in range(UNROLL):
                step(0, cc)
            with eng.Fori(1, n - 1) as i:
                for cc in range(UNROLL):
                    step(i, cc)
            for cc in range(UNROLL):
                step(n - 1, cc)

        def wait(eng, s, value):
            if not isinstance(value, int) or value > 0:
                eng.wait_ge(s, value)

        def channel(i, cc):
            return i * UNROLL + cc

        def known(i, c):
            return not isinstance(i, int) or 0 <= c < C

        def stored_before(t, k):
            return (t - k % O_SLOTS) * (32 // O_SLOTS)

        def tile_loop(eng, step):
            bodies = TILES // T_SLOTS
            for k in range(T_SLOTS):
                step(k, k, 0)
            with eng.Fori(1, bodies - 1) as j:
                for k in range(T_SLOTS):
                    step(j * T_SLOTS + k, k, j)
            for t in range((bodies - 1) * T_SLOTS, TILES):
                step(t, t % T_SLOTS, t // T_SLOTS)

        def bank(k, u):
            return (k % 2) * 4 + 2 * u

        last_slot = (C - 1) % 2
        per_pair = B * HB // PAIRS

        def masked_pair(pair):
            return masked[last_slot][:, pair * per_pair:(pair + 1) * per_pair, 0:S]

        def y_pair(pair):
            return y_sb[last_slot].rearrange("p (i w) -> p i w", w=S)[:, pair * per_pair:(pair + 1) * per_pair, :]

        def mask_pair(pair):
            return mask[:].rearrange("p (i w) -> p i w", w=S)[:, pair * per_pair:(pair + 1) * per_pair, :]

        def row_block_0(slot):
            return x_sb[slot].rearrange("p (b h w) -> p b h w", b=B, h=HB)[:, :, 0, :]

        block = ctx.enter_context(nc.Block())

        @block.sync
        def _(sp):
            sp.dma_start(first_sb, first).then_inc(params_loaded, 16)
            sp.dma_start(col[:], columns).then_inc(params_loaded, 16)
            sp.wait_ge(w_zeroed, 1)
            for k in range(2):
                h = slice(k * ORDER, (k + 1) * ORDER)
                sp.dma_start(w_sb[h, :, h], hidden[h, :].rearrange("p (l n) -> p l n", l=3)
                             ).then_inc(params_loaded, 16)

            def load_x(i, cc, ahead):
                c = channel(i, cc + ahead)
                if not known(i, c):
                    return
                wait(sp, y_done, PAIRS * (c - X_SLOTS) + PAIRS)
                sp.dma_start(x_sb[(cc + ahead) % X_SLOTS], x[bass.ds(c, 1), :, :].rearrange("o p n -> (o p) n")).then_inc(
                    x_loaded[(cc + ahead) % X_SLOTS], 16)

            def load_hankel(i, cc, ahead):
                c = channel(i, cc + ahead)
                if not known(i, c):
                    return
                k = (cc + ahead) % 2
                wait(sp, flipped, c - 1)
                wait(sp, t_lo_done, c - 1)
                src = bass.AP(tensor=g_dram.tensor, offset=c * GLEN, ap=[[1, P], [C * GLEN, 2], [1, S]])
                sp.dma_start(hankel[k], src).then_inc(hankel_loaded[k], 16)

            def store_y(i, cc, behind):
                c = channel(i, cc - behind)
                if not known(i, c):
                    return
                k = (cc - behind) % 2
                wait(sp, y_done, PAIRS * (c + 1))
                sp.dma_start(y_dram[bass.ds(c, 1), :, :].rearrange("o p n -> (o p) n"), y_sb[k]).then_inc(y_stored[k], 16)

            for c in range(X_SLOTS - 1):
                load_x(0, 0, c)
            sp.dma_start(bias_sb[:], bias.to_broadcast([P, C])).then_inc(bias_loaded, 16)
            sp.wait_ge(filt_ready, 1)
            sp.dma_start(g_dram, filt).then_inc(filt_stored, 16)
            sp.wait_ge(filt_stored, 16)
            load_hankel(0, 0, 0)
            load_hankel(0, 0, 1)

            def step(i, cc):
                load_hankel(i, cc, 2)
                load_x(i, cc, X_SLOTS - 1)
                store_y(i, cc, 1)

            channels(sp, step)
            store_y(C // UNROLL - 1, UNROLL, 1)

            for k in range(2):
                sp.wait_ge(y_stored[k], 16 * (C // 2))
            sp.wait_ge(z_done, C - 1)
            sp.wait_ge(z_last_done, PAIRS)
            sp.wait_ge(y_done, PAIRS * C)

            def load_tile(t, k):
                for b in range(2):
                    src = bass.AP(tensor=y_dram.tensor,
                                  offset=(t - k % PAIRS) * (TROWS * B * IMG // PAIRS) + (k % PAIRS * 2 + b) * IMG,
                                  ap=[[P * B * IMG, C], [B * IMG, TROWS], [1, IMG]])
                    sp.dma_start(t_in[k][b * C:(b + 1) * C, :].rearrange("c (r n) -> c r n", r=TROWS),
                                 src).then_inc(t_loaded[k], 16)

            def store_tile(t, k):
                for b in range(2):
                    dst = bass.AP(tensor=out.tensor,
                                  offset=(t - k % PAIRS) * (TROWS * S // PAIRS) + (k % PAIRS * 2 + b) * C * S * S,
                                  ap=[[S * S, C], [P * S, HB], [1, TROWS * S]])
                    sp.dma_start(dst, t_out[k % O_SLOTS][b * C:(b + 1) * C, :].rearrange(
                        "c (h n) -> c h n", h=HB)).then_inc(t_stored[k % O_SLOTS], 16)

            def tile(t, k, j):
                if not isinstance(t, int) or t + T_SLOTS < TILES:
                    sp.wait_ge(t_mm[UNITS - 1], t + 1)
                    load_tile(t + T_SLOTS, k)
                sp.wait_ge(t_act, t + 1)
                sp.wait_ge(t_dve, t + 1)
                store_tile(t, k)

            for k in range(early):
                load_tile(k, k)
            sp.wait_ge(cov_mm, 1)
            for k in range(early, T_SLOTS):
                load_tile(k, k)
            tile_loop(sp, tile)
            for k in range(O_SLOTS):
                sp.wait_ge(t_stored[k], 32 * (TILES // O_SLOTS))

        @block.gpsimd
        def _(pool):
            n_step = [0]

            def chained(ins):
                n_step[0] += 1
                ins.then_inc(pool_step, 1)
                pool.wait_ge(pool_step, n_step[0])

            def split_x(i, cc, ahead):
                c = channel(i, cc + ahead)
                if not known(i, c):
                    return
                k = (cc + ahead) % 2
                wait(pool, x_hi_done, c + 1)
                nc.gpsimd.tensor_tensor(x_lo[k][:], row_block_0((cc + ahead) % X_SLOTS),
                                        x_hi[k][:].bitcast(F32), ALU.subtract).then_inc(x_lo_done, 1)

            nc.gpsimd.memset(w_sb, 0.0).then_inc(w_zeroed, 1)
            nc.gpsimd.iota(pos_i, pattern=[[-1, S]], base=S - 1, channel_multiplier=0)
            chained(nc.gpsimd.iota(chan_i[:], pattern=[[0, 1]], base=0, channel_multiplier=1))
            nc.gpsimd.tensor_copy(pos, pos_i)
            nc.gpsimd.tensor_copy(chan[:], chan_i[:]).then_inc(pos_ready, 1)
            nc.gpsimd.memset(filt, 0.0).then_inc(filt_zeroed, 1)
            nc.gpsimd.memset(small[:], 0.0).then_inc(filt_zeroed, 1)
            split_x(0, 0, 0)
            nc.gpsimd.iota(mask_scratch[0].bitcast(I32).rearrange("p (b h w) -> p b h w", b=B, h=HB),
                           pattern=[[(S * S) % STRIDE, B], [(S * P) % STRIDE, HB], [1, S]],
                           base=0, channel_multiplier=S % STRIDE).then_inc(index_ready, 1)
            for k in range(2):
                nc.gpsimd.memset(masked[k][:, :, S:], 0.0)
            chained(nc.gpsimd.memset(ident[:], 0.0))
            chained(nc.gpsimd.affine_select(out=ident[:], in_=ident[:], compare_op=ALU.not_equal, fill=1.0,
                                            base=0, pattern=[[-1, P]], channel_multiplier=1))
            nc.gpsimd.tensor_scalar(ident15[:], ident[:], 1.5, None, ALU.mult)
            nc.gpsimd.tensor_scalar(ident_eps[:], ident[:], EPS, None, ALU.mult)
            for k in range(2):
                nc.gpsimd.tensor_copy(twice[0:C, k * C:(k + 1) * C], ident[0:C, 0:C])
            nc.gpsimd.memset(cov[:], 0.0)
            nc.gpsimd.memset(halves[:], 0.5).then_inc(ident_ready, 1)
            nc.gpsimd.memset(z_sb[:, C, :], 1.0).then_inc(ident_ready, 1)
            pool.wait_ge(ident_ready, 2)

            def mask_y(i, cc, behind):
                c = channel(i, cc - behind)
                if not known(i, c):
                    return
                k = (cc - behind) % 2
                wait(pool, y_done, PAIRS * (c + 1))
                wait(pool, z_done, c - 1)
                nc.gpsimd.tensor_tensor(masked[k][:, :, 0:S], y_sb[k].rearrange("p (i w) -> p i w", w=S),
                                        mask[:].rearrange("p (i w) -> p i w", w=S),
                                        ALU.mult).then_inc(masked_done, 1)

            def step(i, cc):
                split_x(i, cc, 1)
                mask_y(i, cc, 1)

            channels(pool, step)
            pool.wait_ge(y_done, PAIRS * C - 1)
            pool.wait_ge(z_done, C - 2)
            nc.gpsimd.tensor_tensor(masked_pair(0), y_pair(0), mask_pair(0), ALU.mult).then_inc(masked_done, 1)

        @block.scalar
        def _(act):
            def flip(i, cc, ahead):
                c = channel(i, cc + ahead)
                if not known(i, c):
                    return
                k = (cc + ahead) % 2
                act.wait_ge(hankel_loaded[k], 16 * (c // 2 + 1) if isinstance(c, int)
                            else 16 * (i * (UNROLL // 2) + (cc + ahead) // 2 + 1))
                wait(act, y_mm, PAIRS * (c - 1))
                wait(act, t_lo_done, c - 1)
                nc.scalar.copy(t_f32[k][:], hankel[k][:, :, :P - 1:-1])
                nc.scalar.copy(t_hi[k][:], hankel[k][:, :, ::-1]).then_inc(flipped, 1)

            def round_x(i, cc, ahead):
                c = channel(i, cc + ahead)
                if not known(i, c):
                    return
                k = (cc + ahead) % X_SLOTS
                act.wait_ge(x_loaded[k], 16 * (c // X_SLOTS + 1) if isinstance(c, int)
                            else 16 * (i + (cc + ahead) // X_SLOTS + 1))
                wait(act, v_mm, PAIRS * (c - 1))
                nc.scalar.copy(x_hi[(cc + ahead) % 2][:], row_block_0(k)).then_inc(x_hi_done, 1)

            def round_v(i, cc, pair):
                q = channel(i, cc) * PAIRS + pair
                wait(act, v_mm, q + 1)
                wait(act, y_mm, q - 1)
                nc.scalar.copy(v_f32[pair][:], ps_v[pair][:, :, S:2 * S])
                nc.scalar.copy(v_hi[pair][:], ps_v[pair][:, :, 0:S]).then_inc(v_hi_done, 1)

            act.wait_ge(rate_ready, 1)
            nc.scalar.activation(decay, pos, ACT.Exp, scale=rate[:]).then_inc(decay_ready, 1)
            round_x(0, 0, 0)
            for layer in range(3):
                act.wait_ge(f_dve, layer + 1)
                nc.scalar.activation(hid, arg, ACT.Sin).then_inc(f_sin, 1)
            flip(0, 0, 0)

            def step(i, cc):
                round_x(i, cc, 1)
                round_v(i, cc, 0)
                flip(i, cc, 1)
                round_v(i, cc, 1)

            channels(act, step)

            act.wait_ge(filt_zeroed, 2)
            nc.scalar.activation(small[:, 7:8], small[:, 7:8], ACT.Sqrt)
            act.wait_ge(n_mm, 1)
            nc.scalar.activation(small[:, 1:2], ps[:, 0, 0:1], ACT.Sqrt).then_inc(n_act, 1)
            act.wait_ge(n_act, 1)
            nc.scalar.activation(small[:, 3:4], small[:, 1:2], ACT.Sqrt).then_inc(n_act, 1)
            act.wait_ge(d_ready, 1)

            def tile(t, k, j):
                act.wait_ge(t_mm[0], t + 1)
                wait(act, t_stored[k % O_SLOTS], stored_before(t, k))
                src = ps[:, bank(k, 0):bank(k, 0) + 2, :].rearrange("p r (h w) -> p r h w", h=HB)
                dst = t_out[k % O_SLOTS].rearrange("p (h r w) -> p r h w", h=HB, r=TROWS)[:, 0:2]
                nc.scalar.activation(dst, src, ACT.Identity, bias=small[:, 6:7]).then_inc(t_act, 1)

            tile_loop(act, tile)

        @block.vector
        def _(dve):
            step_sem = ctx.enter_context(nc.semaphore("dve_step"))
            n_step = [0]

            def chained(ins):
                n_step[0] += 1
                ins.then_inc(step_sem, 1)
                dve.wait_ge(step_sem, n_step[0])

            dve.wait_ge(pos_ready, 1)
            step = (MAX_DEC - MIN_DEC) / (C - 1)
            chained(nc.vector.tensor_scalar(rate[0:C, :], chan[0:C, :], -step, -MIN_DEC, ALU.mult, ALU.add))
            chained(nc.vector.tensor_scalar(rate[C:P, :], chan[C:P, :], -step, C * step - MIN_DEC, ALU.mult, ALU.add))
            nc.vector.tensor_scalar(rate[:], rate[:], 1.0 / (S - 1), None, ALU.mult).then_inc(rate_ready, 1)
            dve.wait_ge(params_loaded, 16 * 4)
            for layer in range(3):
                dve.wait_ge(f_mm, layer + 1)
                chained(nc.vector.tensor_scalar(arg, ps[:, 0, 0:S], col[:, layer:layer + 1], col[:, 3:4],
                                                ALU.add, ALU.mult))
                chained(nc.vector.tensor_scalar(turns, arg, 1.0 / TWO_PI, MAGIC, ALU.mult, ALU.add))
                chained(nc.vector.tensor_scalar(turns, turns, MAGIC, None, ALU.subtract))
                for part in (PI_HI, PI_MID, PI_LO):
                    chained(nc.vector.scalar_tensor_tensor(arg, turns, -part, arg, ALU.mult, ALU.add))
                nc.vector.tensor_scalar(arg, arg, PI_BELOW, -PI_BELOW, ALU.min, ALU.max).then_inc(f_dve, 1)
                dve.wait_ge(f_sin, layer + 1)
            dve.wait_ge(decay_ready, 1)
            chained(nc.vector.tensor_scalar(decay[0:C, :], decay[0:C, :], 1.0 / (2 * S), None, ALU.mult))
            dve.wait_ge(filt_zeroed, 1)
            dve.wait_ge(f_mm, 4)
            nc.vector.tensor_tensor(filt[:, 0:S], ps[:, 0, 0:S], decay, ALU.mult).then_inc(filt_ready, 1)
            dve.wait_ge(index_ready, 1)
            idx, near = mask_scratch[1], mask_scratch[2]
            chained(nc.vector.tensor_copy(idx, mask_scratch[0].bitcast(I32)))
            chained(nc.vector.tensor_scalar(near, idx, 1.0 / STRIDE, MAGIC, ALU.mult, ALU.add))
            chained(nc.vector.tensor_scalar(near, near, MAGIC, float(STRIDE), ALU.subtract, ALU.mult))
            chained(nc.vector.tensor_tensor(idx, idx, near, ALU.subtract))
            nc.vector.tensor_scalar(mask[:], idx, 0.0, None, ALU.is_equal).then_inc(mask_ready, 1)

            def split_v(i, cc, pair):
                q = channel(i, cc) * PAIRS + pair
                wait(dve, v_hi_done, q + 1)
                nc.vector.tensor_tensor(v_lo[pair][:], ps_v[pair][:, :, 0:S],
                                        v_hi[pair][:].bitcast(F32), ALU.subtract).then_inc(v_lo_done, 1)

            def split_t(i, cc, ahead):
                c = channel(i, cc + ahead)
                if not known(i, c):
                    return
                k = (cc + ahead) % 2
                wait(dve, flipped, c + 1)
                nc.vector.tensor_tensor(t_lo[k][:], hankel[k][:, :, ::-1], t_hi[k][:].bitcast(F32),
                                        ALU.subtract).then_inc(t_lo_done, 1)

            def finish_y(i, cc, pair):
                c = channel(i, cc)
                if not known(i, c):
                    return
                q = c * PAIRS + pair
                if pair == 0:
                    stored = 16 * (c // 2) if isinstance(c, int) else 16 * (i * (UNROLL // 2) + cc // 2)
                    wait(dve, y_stored[cc % 2], stored)
                    wait(dve, masked_done, c - 1)
                wait(dve, y_mm, q + 1)
                half = slice(pair * 2 * IMG, (pair + 1) * 2 * IMG)
                nc.vector.scalar_tensor_tensor(y_sb[cc % 2][:, half], x_sb[cc % X_SLOTS][:, half],
                                               bias_sb[:, bass.ds(c, 1)],
                                               ps_y[pair].rearrange("p a n -> p (a n)"),
                                               ALU.mult, ALU.add).then_inc(y_done, 1)

            def sum_masked(i, cc, behind):
                c = channel(i, cc - behind)
                if not known(i, c):
                    return
                wait(dve, masked_done, c + 1)
                nc.vector.tensor_reduce(z_sb[:, bass.ds(c, 1), :].rearrange("p o s -> p (o s)"),
                                        masked[(cc - behind) % 2].rearrange("p i (j u) -> p (i j) u", u=STRIDE),
                                        AX_X, ALU.add).then_inc(z_done, 1)

            split_t(0, 0, 0)
            dve.wait_ge(bias_loaded, 16)

            def step(i, cc):
                split_v(i, cc, 0)
                finish_y(i, cc - 1, 1)
                split_t(i, cc, 1)
                sum_masked(i, cc, 2)
                split_v(i, cc, 1)
                finish_y(i, cc, 0)

            channels(dve, step)
            last = C // UNROLL - 1
            sum_masked(last, UNROLL, 2)
            finish_y(last, UNROLL - 1, 1)

            def sum_pair(pair):
                w = per_pair * GROUPS
                nc.vector.tensor_reduce(z_sb[:, C - 1, pair * w:(pair + 1) * w],
                                        masked[last_slot][:, pair * per_pair:(pair + 1) * per_pair, :].rearrange(
                                            "p i (j u) -> p (i j) u", u=STRIDE),
                                        AX_X, ALU.add).then_inc(z_last_done, 1)

            dve.wait_ge(masked_done, C)
            sum_pair(0)
            dve.wait_ge(y_done, PAIRS * C)
            chained(nc.vector.tensor_tensor(masked_pair(1), y_pair(1), mask_pair(1), ALU.mult))
            sum_pair(1)

            dve.wait_ge(cov_mm, 1)
            nc.vector.tensor_copy(sums[0:C, :], ps[0:C, 0, 0:C + 1]).then_inc(sums_ready, 1)
            dve.wait_ge(cov_mm, 2)
            for k in range(2):
                h = slice(k * C, (k + 1) * C)
                chained(nc.vector.scalar_tensor_tensor(cov[h, h], ps[h, 1, 0:C], 1.0 / N_SAMPLES,
                                                       ident_eps[h, h], ALU.mult, ALU.add))
            nc.vector.tensor_scalar(small[:, 5:6], ps[:, 1, C:C + 1], 1.0 / N_SAMPLES, None, ALU.mult)
            chained(nc.vector.tensor_tensor(sq, cov[:], cov[:], ALU.mult))
            nc.vector.tensor_reduce(small[:, 0:1], sq, AX_X, ALU.add).then_inc(n_dve, 1)
            dve.wait_ge(n_act, 1)
            chained(nc.vector.reciprocal(small[:, 2:3], small[:, 1:2]))
            nc.vector.tensor_scalar(ym[0][:], cov[:], small[:, 2:3], None, ALU.mult).then_inc(n_dve, 1)
            dve.wait_ge(n_act, 2)
            chained(nc.vector.reciprocal(small[:, 4:5], small[:, 3:4]))
            n = 1
            for it in range(N_ITER):
                if it == 0:
                    nc.vector.scalar_tensor_tensor(tm, ym[0][:], -0.5, ident15[:], ALU.mult, ALU.add
                                                   ).then_inc(n_dve, 1)
                else:
                    n += 1
                    dve.wait_ge(n_mm, n)
                    nc.vector.scalar_tensor_tensor(tm, ps[:, 1, 0:P], -0.5, ident15[:], ALU.mult, ALU.add
                                                   ).then_inc(n_dve, 1)
                a = (it + 1) % 2
                if it < N_ITER - 1:
                    n += 1
                    dve.wait_ge(n_mm, n)
                    nc.vector.tensor_copy(ym[a][:], ps[:, 2, 0:P])
                    nc.vector.tensor_copy(zm[a][:], ps[:, 3, 0:P]).then_inc(n_dve, 1)
                else:
                    n += 1
                    dve.wait_ge(n_mm, n)
                    nc.vector.tensor_scalar(dmat, ps[:, 3, 0:P], small[:, 4:5], None, ALU.mult).then_inc(n_dve, 1)
            dve.wait_ge(n_mm, n + 1)
            nc.vector.tensor_scalar(small[:, 6:7], ps[:, 1, 0:1], -1.0, None, ALU.mult).then_inc(d_ready, 1)
            dve.wait_ge(d_ready, 1)

            def tile(t, k, j):
                dve.wait_ge(t_mm[1], t + 1)
                wait(dve, t_stored[k % O_SLOTS], stored_before(t, k))
                src = ps[:, bank(k, 1):bank(k, 1) + 2, :].rearrange("p r (h w) -> p r h w", h=HB)
                dst = t_out[k % O_SLOTS].rearrange("p (h r w) -> p r h w", h=HB, r=TROWS)[:, 2:4]
                nc.vector.tensor_scalar(dst, src, small[:, 6:7], None, ALU.add).then_inc(t_dve, 1)

            tile_loop(dve, tile)

        @block.tensor
        def _(pe):
            mm = nc.tensor.matmul
            pe.wait_ge(params_loaded, 16 * 4)
            mm(ps[:, 0, 0:S], first_sb[:, 0:2 * ORDER], first_sb[:, 2 * ORDER:], start=True, stop=True
               ).then_inc(f_mm, 1)
            for layer in range(3):
                pe.wait_ge(f_sin, layer + 1)
                mm(ps[:, 0, 0:S], w_sb[:, layer, :], hid, start=True, stop=True).then_inc(f_mm, 1)
            pe.wait_ge(filt_ready, 1)

            def toeplitz(o, hi, lo, block1, k, f):
                for im in range(2):
                    for m in range(HB):
                        cols = slice(m * P, (m + 1) * P)
                        wide = o[:, im, m * S:(m + 1) * S]
                        mm(wide, hi[:, im, cols], t_hi[k][:, f, :], start=True, stop=False)
                        mm(wide, hi[:, im, cols], t_lo[k][:, f, :], start=False, stop=False)
                        mm(wide, lo[:, im, cols], t_hi[k][:, f, :], start=False, stop=False)
                        last = mm(o[:, im, m * S + P:(m + 1) * S], block1[:, im, cols], t_f32[k][:, f, :],
                                  start=False, stop=True)
                return last

            def make_v(i, cc, pair):
                c = channel(i, cc)
                if not known(i, c):
                    return
                q = c * PAIRS + pair
                if pair == 0:
                    wait(pe, x_lo_done, c + 1)
                    wait(pe, t_lo_done, c + 1)
                wait(pe, v_lo_done, q - 1)
                images = slice(pair * 2, pair * 2 + 2)
                toeplitz(ps_v[pair], x_hi[cc % 2][:, images, :], x_lo[cc % 2][:, images, :],
                         x_sb[cc % X_SLOTS].rearrange("p (b h w) -> p b h w", b=B, h=HB)[:, images, 1, :],
                         cc % 2, 0).then_inc(v_mm, 1)

            def make_y(i, cc, pair):
                q = channel(i, cc) * PAIRS + pair
                wait(pe, v_lo_done, q + 1)
                wait(pe, y_done, q - 1)
                toeplitz(ps_y[pair], v_hi[pair], v_lo[pair], v_f32[pair], cc % 2, 1).then_inc(y_mm, 1)

            make_v(0, 0, 0)

            def step(i, cc):
                make_v(i, cc, 1)
                make_y(i, cc, 0)
                make_v(i, cc + 1, 0)
                make_y(i, cc, 1)

            channels(pe, step)

            pe.wait_ge(z_done, C - 1)
            pe.wait_ge(ident_ready, 2)
            slots = B * HB * GROUPS
            for s in range(slots):
                if s % (slots // PAIRS) == 0:
                    pe.wait_ge(z_last_done, s // (slots // PAIRS) + 1)
                last = mm(ps[0:C, 0, 0:C + 1], z_sb[:, 0:C, s], z_sb[:, :, s],
                          start=(s == 0), stop=(s == slots - 1))
            last.then_inc(cov_mm, 1)
            pe.wait_ge(sums_ready, 1)
            mm(ps[:, 1, 0:C + 1], twice[0:C, :], sums[0:C, :], start=True, stop=True).then_inc(cov_mm, 1)
            pe.wait_ge(n_dve, 1)
            mm(ps[:, 0, 0:1], halves[:], small[:, 0:1], start=True, stop=True).then_inc(n_mm, 1)
            n = 2
            for it in range(N_ITER):
                a = it % 2
                zz = ident if it == 0 else zm[a]
                if it > 0:
                    n += 1
                    pe.wait_ge(n_dve, n)
                    mm(ps[:, 1, 0:P], zz[:], ym[a][:], start=True, stop=True).then_inc(n_mm, 1)
                n += 1
                pe.wait_ge(n_dve, n)
                if it < N_ITER - 1:
                    mm(ps[:, 2, 0:P], ym[a][:], tm, start=True, stop=True)
                mm(ps[:, 3, 0:P], tm, zz[:], start=True, stop=True).then_inc(n_mm, 1)
            pe.wait_ge(n_dve, n + 1)
            mm(ps[:, 1, 0:1], dmat, small[:, 5:6], start=True, stop=True).then_inc(n_mm, 1)
            pe.wait_ge(d_ready, 1)

            def tile(t, k, j):
                pe.wait_ge(t_loaded[k], 32 * (j + 1))
                for u in range(UNITS):
                    wait(pe, t_dve if u else t_act, t - 1)
                    for r in range(2):
                        row = 2 * u + r
                        last = mm(ps[:, bank(k, u) + r, :], dmat, t_in[k][:, row * IMG:(row + 1) * IMG],
                                  start=True, stop=True)
                    last.then_inc(t_mm[u], 1)

            tile_loop(pe, tile)


def kernel(**inputs):
    import numpy as np
    import concourse.bacc as bacc
    from concourse.bass_utils import run_bass_kernel_spmd

    a = {k: np.asarray(v) for k, v in inputs.items()}
    x = a["x"].reshape(B, C, HB, P, S).transpose(1, 3, 0, 2, 4).reshape(C, P, B * IMG)

    def both(name):
        return np.concatenate([a[f"L0_conv_{n}{name}"].reshape(ORDER, -1) for n in "XY"], axis=0)

    arrays = {
        "x": x,
        "first": np.concatenate([a["L0_conv_Xw1"], a["L0_conv_Yw1"], a["L0_conv_z"][0, ::-1, :].T], axis=1),
        "hidden": np.concatenate([both("w2"), both("w3"), both("wo")], axis=1),
        "columns": np.concatenate([both("b1"), both("b2"), both("b3"), both("freq")], axis=1),
        "bias": a["L0_conv_bias"].reshape(1, C),
    }
    arrays = {k: np.ascontiguousarray(v) for k, v in arrays.items()}
    nc = bacc.Bacc("TRN2", target_bir_lowering=False, num_devices=1)
    aps = [nc.dram_tensor(k, v.shape, mybir.dt.from_np(v.dtype), kind="ExternalInput").ap()
           for k, v in arrays.items()]
    out = nc.dram_tensor("out", [B, C, S, S], F32, kind="ExternalOutput").ap()
    conv_whiten(nc, *aps, out)
    r = run_bass_kernel_spmd(nc, [arrays], core_ids=[0])
    return r.results[0]["out"]
```
